# Optimizing a Trainium2 kernel written in Bass

```python
import numpy as np
import jax
import jax.numpy as jnp

def _softmax(x, axis=-1):
    return jax.nn.softmax(x, axis=axis)
def _gelu(x):
    return jax.nn.gelu(x, approximate=True)
def _silu(x):
    return jax.nn.silu(x)
def _sigmoid(x):
    return jax.nn.sigmoid(x)
def _layernorm(x, axis=-1, eps=1e-5):
    m = jnp.mean(x, axis=axis, keepdims=True)
    v = jnp.var(x, axis=axis, keepdims=True)
    return (x - m) / jnp.sqrt(v + eps)
def _scatter_add(tgt, idx, src, axis=0):
    return tgt.at[idx].add(src)
def _segment_sum(src, seg, n):
    return jax.ops.segment_sum(src, seg, n)

kernel_name = 'mk_conv_seq_d2_conv_nchw512_3912d8'

def setup_inputs(seed: int = 0):
    np.random.seed(seed)
    _w = jnp.asarray
    def _rec_inputs():
        import jax
        import jax.numpy as jnp
        _gk = jax.random.key(seed)
        x = -0.0002928 + 1 * jax.random.normal(jax.random.fold_in(_gk, 1), (8, 512, 32, 32), jnp.float32)
        return x
    x = _rec_inputs()
    def _L0_conv_setup():
        import jax, jax.numpy as jnp
        import numpy as np
        GH, GW = (7, 7)
        LN_EPS = 1e-05
        NEG = -1000000000.0

        def _adaptive_avg_pool2d(x, oh, ow):
            H, W = (x.shape[-2], x.shape[-1])

            def b(i, n, o):
                return (int(np.floor(i * n / o)), int(np.ceil((i + 1) * n / o)))
            rows = jnp.stack([x[..., b(i, H, oh)[0]:b(i, H, oh)[1], :].mean(axis=-2) for i in range(oh)], axis=-2)
            out = jnp.stack([rows[..., b(j, W, ow)[0]:b(j, W, ow)[1]].mean(axis=-1) for j in range(ow)], axis=-1)
            return out

        def _layernorm(y, gamma, beta):
            mu = y.mean(axis=-1, keepdims=True)
            var = jnp.mean(jnp.square(y - mu), axis=-1, keepdims=True)
            return (y - mu) * jax.lax.rsqrt(var + LN_EPS) * gamma + beta
        key = jax.random.key(seed)
        ks = jax.random.split(key, 16)
        B, C, H, W = (8, 512, 32, 32)
        heads = 8
        s = 0.02
        f32 = jnp.float32
        return {'x': jax.random.normal(ks[0], (B, C, H, W), f32), 'Wq': jax.random.normal(ks[1], (C, C), f32) * s, 'bq': jnp.zeros((C,), f32), 'Wk': jax.random.normal(ks[2], (C, C), f32) * s, 'bk': jnp.zeros((C,), f32), 'Wv': jax.random.normal(ks[3], (C, C), f32) * s, 'bv': jnp.zeros((C,), f32), 'Wo': jax.random.normal(ks[4], (C, C), f32) * s, 'bo': jnp.zeros((C,), f32), 'Wsp': jax.random.normal(ks[5], (heads, C), f32) * s, 'bsp': jnp.zeros((heads,), f32), 'Wse1': jax.random.normal(ks[6], (C // 16, C), f32) * s, 'bse1': jnp.zeros((C // 16,), f32), 'Wse2': jax.random.normal(ks[7], (C, C // 16), f32) * s, 'bse2': jnp.zeros((C,), f32), 'gamma': jnp.ones((C,), f32), 'beta': jnp.zeros((C,), f32)}
    _L0_conv_all = _L0_conv_setup()
    _L0_conv_in = {k: v for k, v in _L0_conv_all.items() if k in ('Wq', 'bq', 'Wk', 'bk', 'Wv', 'bv', 'Wo', 'bo', 'Wsp', 'bsp', 'Wse1', 'bse1', 'Wse2', 'bse2', 'gamma', 'beta', )}
    del _L0_conv_all

    def _L1_conv_setup():
        import jax, jax.numpy as jnp
        import numpy as np
        B, C, H, W = (8, 512, 32, 32)
        HEAD = 2 * 4
        QK_DIM = 256
        DH = QK_DIM // HEAD

        def _conv1x1(x, Wt, b):
            return jnp.einsum('oc,bchw->bohw', Wt, x) + b[None, :, None, None]

        def _mish(x):
            return x * jnp.tanh(jax.nn.softplus(x))
        key = jax.random.key(seed)
        ks = jax.random.split(key, 12)
        s = 0.05
        return {'x': jax.random.normal(ks[0], (B, C, H, W), jnp.float32), 'PE': jax.random.normal(ks[1], (DH, H, W), jnp.float32) * s, 'Wq': jax.random.normal(ks[2], (QK_DIM, C), jnp.float32) * s, 'bq': jnp.zeros((QK_DIM,), jnp.float32), 'Wk': jax.random.normal(ks[3], (QK_DIM, C), jnp.float32) * s, 'bk': jnp.zeros((QK_DIM,), jnp.float32), 'Wv': jax.random.normal(ks[4], (C, C), jnp.float32) * s, 'bv': jnp.zeros((C,), jnp.float32), 'W1': jax.random.normal(ks[5], (C, C), jnp.float32) * s, 'b1': jnp.zeros((C,), jnp.float32), 'W2': jax.random.normal(ks[6], (C, C), jnp.float32) * s, 'b2': jnp.zeros((C,), jnp.float32)}
    _L1_conv_all = _L1_conv_setup()
    _L1_conv_in = {k: v for k, v in _L1_conv_all.items() if k in ('PE', 'Wq', 'bq', 'Wk', 'bk', 'Wv', 'bv', 'W1', 'b1', 'W2', 'b2', )}
    del _L1_conv_all

    return {
        "x": x,
        "L0_conv_Wq": _L0_conv_in["Wq"],
        "L0_conv_bq": _L0_conv_in["bq"],
        "L0_conv_Wk": _L0_conv_in["Wk"],
        "L0_conv_bk": _L0_conv_in["bk"],
        "L0_conv_Wv": _L0_conv_in["Wv"],
        "L0_conv_bv": _L0_conv_in["bv"],
        "L0_conv_Wo": _L0_conv_in["Wo"],
        "L0_conv_bo": _L0_conv_in["bo"],
        "L0_conv_Wsp": _L0_conv_in["Wsp"],
        "L0_conv_bsp": _L0_conv_in["bsp"],
        "L0_conv_Wse1": _L0_conv_in["Wse1"],
        "L0_conv_bse1": _L0_conv_in["bse1"],
        "L0_conv_Wse2": _L0_conv_in["Wse2"],
        "L0_conv_bse2": _L0_conv_in["bse2"],
        "L0_conv_gamma": _L0_conv_in["gamma"],
        "L0_conv_beta": _L0_conv_in["beta"],
        "L1_conv_PE": _L1_conv_in["PE"],
        "L1_conv_Wq": _L1_conv_in["Wq"],
        "L1_conv_bq": _L1_conv_in["bq"],
        "L1_conv_Wk": _L1_conv_in["Wk"],
        "L1_conv_bk": _L1_conv_in["bk"],
        "L1_conv_Wv": _L1_conv_in["Wv"],
        "L1_conv_bv": _L1_conv_in["bv"],
        "L1_conv_W1": _L1_conv_in["W1"],
        "L1_conv_b1": _L1_conv_in["b1"],
        "L1_conv_W2": _L1_conv_in["W2"],
        "L1_conv_b2": _L1_conv_in["b2"],
    }

def reference(x, L0_conv_Wq, L0_conv_bq, L0_conv_Wk, L0_conv_bk, L0_conv_Wv, L0_conv_bv, L0_conv_Wo, L0_conv_bo, L0_conv_Wsp, L0_conv_bsp, L0_conv_Wse1, L0_conv_bse1, L0_conv_Wse2, L0_conv_bse2, L0_conv_gamma, L0_conv_beta, L1_conv_PE, L1_conv_Wq, L1_conv_bq, L1_conv_Wk, L1_conv_bk, L1_conv_Wv, L1_conv_bv, L1_conv_W1, L1_conv_b1, L1_conv_W2, L1_conv_b2):
    import jax
    import jax.numpy as jnp
    def _L0_conv_ref(x, Wq, bq, Wk, bk, Wv, bv, Wo, bo, Wsp, bsp, Wse1, bse1, Wse2, bse2, gamma, beta):
        import jax, jax.numpy as jnp
        import numpy as np
        GH, GW = (7, 7)
        LN_EPS = 1e-05
        NEG = -1000000000.0

        def _adaptive_avg_pool2d(x, oh, ow):
            H, W = (x.shape[-2], x.shape[-1])

            def b(i, n, o):
                return (int(np.floor(i * n / o)), int(np.ceil((i + 1) * n / o)))
            rows = jnp.stack([x[..., b(i, H, oh)[0]:b(i, H, oh)[1], :].mean(axis=-2) for i in range(oh)], axis=-2)
            out = jnp.stack([rows[..., b(j, W, ow)[0]:b(j, W, ow)[1]].mean(axis=-1) for j in range(ow)], axis=-1)
            return out

        def _layernorm(y, gamma, beta):
            mu = y.mean(axis=-1, keepdims=True)
            var = jnp.mean(jnp.square(y - mu), axis=-1, keepdims=True)
            return (y - mu) * jax.lax.rsqrt(var + LN_EPS) * gamma + beta
        B, C, H, W = x.shape
        heads = Wsp.shape[0]
        d = C // heads
        N = H * W
        sp = jnp.einsum('bchw,nc->bnhw', x, Wsp) + bsp[None, :, None, None]
        m = jax.nn.sigmoid(sp)
        mg = _adaptive_avg_pool2d(m, GH, GW)
        mg = (mg > 0.5).astype(x.dtype)
        ih = np.floor(np.arange(H) * GH / H).astype(np.int32)
        iw = np.floor(np.arange(W) * GW / W).astype(np.int32)
        mask = mg[..., ih[:, None], iw[None, :]]
        pooled = x.mean(axis=(2, 3))
        h1 = jax.nn.relu(pooled @ Wse1.T + bse1)
        cw = jax.nn.sigmoid(h1 @ Wse2.T + bse2)
        xf = (x * cw[:, :, None, None]).reshape(B, C, N).transpose(0, 2, 1)

        def heads_split(t):
            return t.reshape(B, N, heads, d).transpose(0, 2, 1, 3)
        Q = heads_split(xf @ Wq.T + bq)
        K = heads_split(xf @ Wk.T + bk)
        V = heads_split(xf @ Wv.T + bv)
        scores = jnp.einsum('bhnd,bhmd->bhnm', Q, K) / d ** 0.5
        mf = mask.reshape(B, heads, N)
        bias = (1.0 - mf[:, :, :, None] * mf[:, :, None, :]) * NEG
        w = jax.nn.softmax(scores + bias, axis=-1)
        attn = jnp.einsum('bhnm,bhmd->bhnd', w, V)
        attn = attn.transpose(0, 2, 1, 3).reshape(B, N, C)
        attn = attn @ Wo.T + bo
        y = _layernorm(xf + attn, gamma, beta)
        return y.transpose(0, 2, 1).reshape(B, C, H, W)

    def _L1_conv_ref(x, PE, Wq, bq, Wk, bk, Wv, bv, W1, b1, W2, b2):
        import jax, jax.numpy as jnp
        import numpy as np
        B, C, H, W = (8, 512, 32, 32)
        HEAD = 2 * 4
        QK_DIM = 256
        DH = QK_DIM // HEAD

        def _conv1x1(x, Wt, b):
            return jnp.einsum('oc,bchw->bohw', Wt, x) + b[None, :, None, None]

        def _mish(x):
            return x * jnp.tanh(jax.nn.softplus(x))
        b, c, h, w = x.shape
        n = h * w
        dh = DH
        ch = c // HEAD
        q = _conv1x1(x, Wq, bq).reshape(b, HEAD, dh, h, w) + PE
        k = _conv1x1(x, Wk, bk).reshape(b, HEAD, dh, h, w) + PE
        v = _conv1x1(x, Wv, bv).reshape(b, HEAD, ch, h, w)
        q = q.reshape(b, HEAD, dh, n).transpose(0, 1, 3, 2)
        k = k.reshape(b, HEAD, dh, n)
        v = v.reshape(b, HEAD, ch, n).transpose(0, 1, 3, 2)
        scale = 1.0 / jnp.sqrt(jnp.float32(dh))
        qk = jnp.einsum('bhnd,bhdm->bhnm', q, k) * scale
        qk = jax.nn.softmax(qk, axis=2)
        out = jnp.einsum('bhnm,bhmc->bhnc', qk, v)
        out = out.transpose(0, 1, 3, 2).reshape(b, c, h, w)
        out = _conv1x1(_mish(_conv1x1(out, W1, b1)), W2, b2) + x
        return out

    def _gn(v, G=32, eps=1e-5):
        B_, C_, H_, W_ = v.shape
        g = v.reshape(B_, G, C_ // G, H_, W_)
        m = jnp.mean(g, axis=(2, 3, 4), keepdims=True)
        s = jnp.var(g, axis=(2, 3, 4), keepdims=True)
        return ((g - m) / jnp.sqrt(s + eps)).reshape(v.shape)

    def _ln_c(v, eps=1e-6):
        m = jnp.mean(v, axis=1, keepdims=True)
        s = jnp.var(v, axis=1, keepdims=True)
        return (v - m) / jnp.sqrt(s + eps)

    def _ln_t(v, eps=1e-5):
        m = jnp.mean(v, axis=-1, keepdims=True)
        s = jnp.var(v, axis=-1, keepdims=True)
        return (v - m) / jnp.sqrt(s + eps)

    def _to_tokens(v):
        B_, C_, H_, W_ = v.shape
        return v.reshape(B_, C_, H_ * W_).transpose(0, 2, 1)
    def _from_tokens(t, like):
        B_, C_, H_, W_ = like.shape
        return t.transpose(0, 2, 1).reshape(B_, C_, H_, W_)

    x = _L0_conv_ref(x, L0_conv_Wq, L0_conv_bq, L0_conv_Wk, L0_conv_bk, L0_conv_Wv, L0_conv_bv, L0_conv_Wo, L0_conv_bo, L0_conv_Wsp, L0_conv_bsp, L0_conv_Wse1, L0_conv_bse1, L0_conv_Wse2, L0_conv_bse2, L0_conv_gamma, L0_conv_beta)
    x = _L1_conv_ref(x, L1_conv_PE, L1_conv_Wq, L1_conv_bq, L1_conv_Wk, L1_conv_bk, L1_conv_Wv, L1_conv_bv, L1_conv_W1, L1_conv_b1, L1_conv_W2, L1_conv_b2)
    return x


_drawn_inputs = setup_inputs


def setup_inputs(seed=0):
    import zlib

    import numpy as np

    out = dict(_drawn_inputs(seed))
    spreads = {'L0_conv_bq': (0.0, 0.8),
     'L0_conv_bk': (0.0, 0.8),
     'L0_conv_bv': (0.0, 0.1),
     'L0_conv_bo': (0.0, 0.1),
     'L0_conv_bsp': (0.0, 0.8),
     'L0_conv_bse1': (0.0, 0.8),
     'L0_conv_bse2': (0.0, 0.1),
     'L0_conv_gamma': (1.0, 0.2),
     'L0_conv_beta': (0.0, 0.1),
     'L1_conv_bq': (0.0, 0.8),
     'L1_conv_bk': (0.0, 0.1),
     'L1_conv_bv': (0.0, 0.1),
     'L1_conv_b1': (0.0, 0.1),
     'L1_conv_b2': (0.0, 0.1)}
    factors = {'L0_conv_Wq': 8.0,
     'L0_conv_Wk': 8.0,
     'L0_conv_Wv': 5.599,
     'L0_conv_Wsp': 8.0,
     'L0_conv_Wse1': 8.0,
     'L0_conv_Wse2': 8.0,
     'L1_conv_PE': 6.72}
    for name, (base, spread) in spreads.items():
        noise = np.random.default_rng([zlib.crc32(name.encode()), seed]).standard_normal(out[name].shape)
        drawn = base * np.exp(spread * noise) if base else spread * noise
        out[name] = jnp.asarray(drawn.astype(out[name].dtype))
    for name, factor in factors.items():
        out[name] = (out[name] * factor).astype(out[name].dtype)
    return out
```

```python
from contextlib import ExitStack

import concourse.bass as bass
from concourse import mybir

F32 = mybir.dt.float32
ALU = mybir.AluOpType
ACT = mybir.ActivationFunctionType
AX_X = mybir.AxisListType.X

P = 128
B, C, H, W = 8, 512, 32, 32
N = H * W
HALF = 512
NH = N // HALF
CC = C // P
HEADS = 8
PAIRS = HEADS // 2
D = C // HEADS
NT = N // P
TILES = 2 * NT
SE = C // 16
G = 7
NEG = -1000000000.0
DQ = 32
QS1 = 2 * DQ
SCALE0 = D ** -0.5
SCALE1 = 1.0 / float(DQ) ** 0.5
MISH_TOP = 20.0

V0 = {name: i * CC for i, name in enumerate(["bq", "bk", "bv", "bo", "bse2", "gamma", "beta"])}
V1 = {name: i * CC for i, name in enumerate(["bqk", "b1", "b2"])}


def bins(n):
    return [(i * n // G, -(-(i + 1) * n // G)) for i in range(G)]


def spread(n):
    cell = [i * G // n for i in range(n)]
    return [(cell.index(g), n - cell[::-1].index(g)) for g in range(G)]


def layer0(nc, x, w_qkv, w_out, vec, w_sp, b_sp, w_se1, b_se1, w_se2, ident_d, mask_d, y):
    with ExitStack() as ctx:
        def sb(name, shape):
            return ctx.enter_context(nc.sbuf_tensor(name, shape, F32))

        def ps(name, shape):
            return ctx.enter_context(nc.psum_tensor(name, shape, F32))

        def sem(name):
            return ctx.enter_context(nc.semaphore(name))

        ident = sb("ident0", [P, P])
        mean_w = sb("mean_w", [P, P])
        wo = sb("wo", [P, CC, C])
        vecs = sb("vecs0", [P, len(V0) * CC])
        bq8 = sb("bq8", [P, CC])
        eps = sb("eps", [P, 1])
        wsp = sb("wsp", [P, CC, HEADS])
        bsp = sb("bsp", [HEADS, 2])
        wse1 = sb("wse1", [P, CC, SE])
        bse1 = sb("bse1", [SE, 1])
        wse2 = sb("wse2", [SE, C])
        wpair = sb("wpair0", [P, CC, 3 * P])
        xraw = sb("xraw", [P, CC, N])
        xf = sb("xf", [P, CC, N])
        attn = sb("attn0", [P, CC, N])
        yt = sb("yt", [P, CC, N])
        rstd = sb("rstd", [P, N])
        gate = sb("gate", [HEADS, N])
        rows = sb("rows", [HEADS, G, W])
        cells = sb("cells", [HEADS, G, G])
        wide = sb("wide", [HEADS, G, W])
        mrow = sb("mrow", [HEADS, 2, N])
        pooled = sb("pooled", [P, CC])
        hid = sb("hid", [SE, 1])
        sez = sb("sez", [P, CC])
        cw = sb("cw", [P, CC])
        qx = [sb(f"qx{j}", [D + 2, N]) for j in range(2)]
        kx = [sb(f"kx{j}", [D + 2, N]) for j in range(2)]
        vt = sb("vt0", [P, NT, P])
        prob = sb("prob", [P, 2, N])
        pt = sb("pt", [P, 2, NT, HALF])
        nmax = sb("nmax0", [P, TILES])
        zsum = sb("zsum0", [P, TILES])
        zinv = sb("zinv0", [P, TILES])
        zrow = sb("zrow", [P, HALF])

        ps_s = [ps(f"ps_s{i}", [P, N]) for i in range(2)]
        ps_t = [ps(f"ps_t{i}", [P, HALF]) for i in range(2)]
        ps_o = ps("ps_o", [P, HALF])
        ps_z = ps("ps_z", [P, HALF])

        const_in = sem("const_in")
        const_ok = sem("const_ok")
        x_in = sem("x_in")
        w_in = sem("w_in")
        mask_out = sem("mask_out")
        mask_in = sem("mask_in")
        y_out = sem("y_out")
        sp_ps = sem("sp_ps")
        sp_e = sem("sp_e")
        mask_ok = sem("mask_ok")
        pool_ok = sem("pool_ok")
        se1_ps = sem("se1_ps")
        hid_ok = sem("hid_ok")
        se2_ps = sem("se2_ps")
        sez_ok = sem("sez_ok")
        see_ok = sem("see_ok")
        cw_ok = sem("cw_ok")
        xf_ok = sem("xf_ok")
        q_ps, k_ps, v_ps = sem("q_ps"), sem("k_ps"), sem("v_ps")
        qk_ok = sem("qk_ok")
        v_ok = sem("v_ok")
        s_ps = sem("s_ps")
        max_ok = sem("max_ok")
        exp_ok = sem("exp_ok")
        t_ps = sem("t_ps")
        pt_ok = sem("pt_ok")
        zinv_ok = sem("zinv_ok")
        o_ps = sem("o_ps")
        zrow_ok = sem("zrow_ok")
        at_ok = sem("at_ok")
        ln_ps = sem("ln_ps")
        y_ok = sem("y_ok")
        cen_ok = sem("cen_ok")
        sq_ok = sem("sq_ok")
        std_ok = sem("std_ok")
        rstd_ok = sem("rstd_ok")
        nrm_ok = sem("nrm_ok")
        res_ok = sem("res_ok")
        place_ok = sem("place_ok")
        dchain = sem("dchain0")
        CONSTS = 9

        def vec_at(name, c):
            return vecs[:, V0[name] + c:V0[name] + c + 1]

        with nc.Block() as block:

            @block.sync
            def _(sp):
                for dst, src in ((ident, ident_d), (wo, w_out), (vecs, vec), (wsp, w_sp), (bsp[:, 0:1], b_sp),
                                 (wse1, w_se1), (bse1, b_se1), (wse2, w_se2)):
                    sp.dma_start(dst[:] if dst is not bsp else dst, src).then_inc(const_in, 16)
                sp.dma_start(xraw[:], x[0]).then_inc(x_in, 16)
                sp.dma_start(wpair[:], w_qkv[0]).then_inc(w_in, 16)
                sp.wait_ge(const_ok, 1)
                sp.sem_inc(y_out, 1)
                with sp.Fori(0, B) as b:
                    nxt = sp.snap((b + 1) % B)
                    sp.wait_ge(mask_ok, b + 1)
                    sp.dma_start(mask_d, mrow[:]).then_inc(mask_out, 16)
                    sp.wait_ge(mask_out, (b + 1) * 16)
                    sp.wait_ge(xf_ok, b + 1)
                    sp.wait_ge(sp_ps, b + 1)
                    sp.dma_start(xraw[:], x[bass.ds(nxt, 1)].rearrange("o p c n -> (o p) c n")).then_inc(x_in, 16)
                    with sp.Fori(0, PAIRS) as p:
                        nxt_pair = sp.snap((p + 1) % PAIRS)
                        sp.wait_ge(exp_ok, (b * PAIRS + p) * TILES + 1)
                        sp.wait_ge(y_out, b * CC * 16 + 1)
                        for j in range(2):
                            one = mask_d[bass.ds(p * 2 + j, 1)].rearrange("o r n -> (o r) n")
                            sp.dma_start(qx[j][D + 1:D + 2, :], one[0:1, :]).then_inc(mask_in, 16)
                            sp.dma_start(kx[j][D:D + 2, :], one).then_inc(mask_in, 16)
                        sp.wait_ge(v_ps, b * PAIRS + p + 1)
                        sp.dma_start(wpair[:], w_qkv[bass.ds(nxt_pair, 1)]
                                     .rearrange("o p c n -> (o p) c n")).then_inc(w_in, 16)
                    for c in range(CC):
                        sp.wait_ge(res_ok, b * CC + c + 1)
                        sp.dma_start(y[bass.ds(b, 1), :, c, :].rearrange("o p n -> (o p) n"),
                                     yt[:, c, :]).then_inc(y_out, 16)
                sp.wait_ge(y_out, B * CC * 16 + 1)
                sp.wait_ge(x_in, (B + 1) * 16)
                sp.wait_ge(w_in, (B * PAIRS + 1) * 16)

            @block.tensor
            def _(pe):
                pe.wait_ge(const_in, 8 * 16)
                pe.wait_ge(const_ok, 1)
                with pe.Fori(0, B) as b:
                    pe.wait_ge(x_in, (b + 1) * 16)
                    pe.wait_ge(nrm_ok, b + 1)
                    for g in range(NH):
                        for c in range(CC):
                            mm = pe.matmul(ps_s[0][0:HEADS, g * HALF:(g + 1) * HALF], wsp[:, c, :],
                                           xraw[:, c, g * HALF:(g + 1) * HALF], start=c == 0, stop=c == CC - 1)
                    mm.then_inc(sp_ps, 1)
                    pe.wait_ge(pool_ok, b + 1)
                    for c in range(CC):
                        mm = pe.matmul(ps_t[0][0:SE, 0:1], wse1[:, c, :], pooled[:, c:c + 1],
                                       start=c == 0, stop=c == CC - 1)
                    mm.then_inc(se1_ps, 1)
                    pe.wait_ge(hid_ok, b + 1)
                    for c in range(CC):
                        mm = pe.matmul(ps_t[1][:, c:c + 1], wse2[:, c * P:(c + 1) * P], hid[:],
                                       start=True, stop=True)
                    mm.then_inc(se2_ps, 1)
                    with pe.Fori(0, PAIRS) as p:
                        it = pe.snap(b * PAIRS + p)
                        pe.wait_ge(xf_ok, b + 1)
                        pe.wait_ge(sp_e, b + 1)
                        pe.wait_ge(w_in, (it + 1) * 16)
                        pe.wait_ge(exp_ok, it * TILES + 1)
                        for k, (dst, done) in enumerate(((ps_s[0], q_ps), (ps_s[1], k_ps))):
                            for g in range(NH):
                                for c in range(CC):
                                    mm = pe.matmul(dst[:, g * HALF:(g + 1) * HALF], wpair[:, c, k * P:(k + 1) * P],
                                                   xf[:, c, g * HALF:(g + 1) * HALF], start=c == 0, stop=c == CC - 1)
                            mm.then_inc(done, 1)
                        pe.wait_ge(qk_ok, it * 4 + 2)
                        for m in range(NT):
                            for c in range(CC):
                                mm = pe.matmul(ps_s[0][:, m * P:(m + 1) * P], xf[:, c, m * P:(m + 1) * P],
                                               wpair[:, c, 2 * P:3 * P], start=c == 0, stop=c == CC - 1)
                        mm.then_inc(v_ps, 1)
                        pe.wait_ge(mask_in, (it + 1) * 64)
                        pe.wait_ge(qk_ok, it * 4 + 4)
                        pe.wait_ge(v_ok, it + 1)

                        def scores(i):
                            j, t = divmod(i, NT)
                            if i >= 2:
                                pe.wait_ge(exp_ok, it * TILES + i)
                            for g in range(NH):
                                mm = pe.matmul(ps_s[i % 2][:, g * HALF:(g + 1) * HALF],
                                               qx[j][:, t * P:(t + 1) * P], kx[j][:, g * HALF:(g + 1) * HALF],
                                               start=True, stop=True)
                            mm.then_inc(s_ps, 1)

                        def turn(i):
                            pe.wait_ge(exp_ok, it * TILES + i + 2)
                            for h in range(2):
                                pe.wait_ge(pt_ok, (it * TILES + i) * 2 + h + 1)
                                for k in range(4):
                                    m = 4 * h + k
                                    mm = pe.transpose(ps_t[h][:, k * P:(k + 1) * P],
                                                      prob[:, i % 2, m * P:(m + 1) * P], ident[:])
                                mm.then_inc(t_ps, 1)

                        def values(i):
                            j, g = divmod(i // 4, 2)
                            pe.wait_ge(pt_ok, (it * TILES + i) * 2 + 4)
                            pe.wait_ge(at_ok, it * 4 + i // 4 + 1)
                            lanes = slice(D * j, D * j + D)
                            for m in range(NT):
                                pe.matmul(ps_o[lanes, :], vt[:, m, D * j:D * j + D], pt[:, g, m, :],
                                          start=m == 0, stop=m == NT - 1)
                            pe.wait_ge(zinv_ok, it * TILES + i + 1)
                            for k in range(4):
                                mm = pe.matmul(ps_z[lanes, k * P:(k + 1) * P],
                                               zinv[:, i - 3 + k:i - 2 + k].broadcast_to([P, D]), ident[:],
                                               start=True, stop=True)
                            mm.then_inc(o_ps, 1)

                        scores(0)
                        for i in range(TILES):
                            if i + 1 < TILES:
                                scores(i + 1)
                            turn(i)
                            if i % 4 == 0 and i:
                                values(i - 1)
                        values(TILES - 1)
                    pe.wait_ge(at_ok, (b + 1) * 4 * PAIRS + 1)
                    for o in range(CC):
                        pe.wait_ge(y_ok, b * CC + max(o - 1, 0) + 1)
                        for g in range(NH):
                            for c in range(CC):
                                mm = pe.matmul(ps_s[o % 2][:, g * HALF:(g + 1) * HALF], wo[:, c, o * P:(o + 1) * P],
                                               attn[:, c, g * HALF:(g + 1) * HALF], start=c == 0, stop=c == CC - 1)
                        mm.then_inc(ln_ps, 1)
                    for k, (src, ready, n) in enumerate(((yt, y_ok, 1), (attn, sq_ok, 0))):
                        pe.wait_ge(ready, (b + 1) * CC + n)
                        for g in range(NH):
                            for c in range(CC):
                                mm = pe.matmul(ps_s[k][:, g * HALF:(g + 1) * HALF], mean_w[:],
                                               src[:, c, g * HALF:(g + 1) * HALF], start=c == 0, stop=c == CC - 1)
                        mm.then_inc(ln_ps, 1)

            @block.scalar
            def _(act):
                act.sem_inc(exp_ok, 1)
                act.sem_inc(nrm_ok, 1)
                act.wait_ge(const_in, 8 * 16)
                act.wait_ge(const_ok, 1)
                with act.Fori(0, B) as b:
                    act.wait_ge(se1_ps, b + 1)
                    act.activation(hid[:], ps_t[0][0:SE, 0:1], ACT.Relu, bias=bse1[:], scale=1.0 / N).then_inc(hid_ok, 1)
                    act.wait_ge(sez_ok, b + 1)
                    act.activation(sez[:], sez[:], ACT.Exp, scale=-1.0).then_inc(see_ok, 1)
                    act.wait_ge(cw_ok, b + 1)
                    for c in range(CC):
                        last = act.activation(xf[:, c, :], xraw[:, c, :], ACT.Identity, scale=cw[:, c:c + 1])
                    last.then_inc(xf_ok, 1)
                    act.wait_ge(sp_ps, b + 1)
                    act.activation(gate[:], ps_s[0][0:HEADS, :], ACT.Exp, bias=bsp[:, 1:2], scale=-1.0).then_inc(sp_e, 1)
                    with act.Fori(0, PAIRS) as p:
                        it = act.snap(b * PAIRS + p)
                        act.wait_ge(q_ps, it + 1)
                        for j in range(2):
                            act.activation(qx[j][0:D, :], ps_s[0][D * j:D * j + D, :], ACT.Identity,
                                           bias=bq8[D * j:D * j + D, bass.ds(p, 1)], scale=SCALE0).then_inc(qk_ok, 1)
                        act.wait_ge(k_ps, it + 1)
                        for j in range(2):
                            act.activation(kx[j][0:D, :], ps_s[1][D * j:D * j + D, :], ACT.Identity,
                                           bias=vecs[D * j:D * j + D, bass.ds(p + V0["bk"], 1)]).then_inc(qk_ok, 1)

                        def exps(i):
                            act.wait_ge(max_ok, it * TILES + i + 1)
                            if i >= 2:
                                act.wait_ge(t_ps, (it * TILES + i) * 2 - 2)
                            act.activation(prob[:, i % 2, :], ps_s[i % 2][:], ACT.Exp, bias=nmax[:, i:i + 1],
                                           accum_out=zsum[:, i:i + 1]).then_inc(exp_ok, 1)

                        def copy_t(i):
                            act.wait_ge(t_ps, (it * TILES + i) * 2 + 1)
                            g = i // 4 % 2
                            act.activation(pt[:, g, 0:4, i % 4 * P:(i % 4 + 1) * P],
                                           ps_t[0][:].rearrange("p (m n) -> p m n", m=4),
                                           ACT.Identity).then_inc(pt_ok, 1)
                            act.wait_ge(t_ps, (it * TILES + i) * 2 + 2)
                            act.activation(pt[:, g, 4:8, i % 4 * P:(i % 4 + 1) * P],
                                           ps_t[1][:].rearrange("p (m n) -> p m n", m=4),
                                           ACT.Identity).then_inc(pt_ok, 1)

                        def copy_z(i):
                            j = i // NT
                            act.wait_ge(o_ps, it * 4 + i // 4 + 1)
                            act.activation(zrow[D * j:D * j + D, :], ps_z[D * j:D * j + D, :],
                                           ACT.Identity).then_inc(zrow_ok, 1)

                        exps(0)
                        for i in range(TILES):
                            if i + 1 < TILES:
                                exps(i + 1)
                            copy_t(i)
                            if i % 4 == 0 and i:
                                copy_z(i - 1)
                        copy_z(TILES - 1)
                    for c in range(CC):
                        act.wait_ge(cen_ok, b * CC + c + 1)
                        act.activation(attn[:, c, :], yt[:, c, :], ACT.Square).then_inc(sq_ok, 1)
                    act.wait_ge(ln_ps, (b + 1) * (CC + 2))
                    act.activation(rstd[:], ps_s[1][:], ACT.Sqrt, bias=eps[:]).then_inc(std_ok, 1)
                    for c in range(CC):
                        act.wait_ge(rstd_ok, b * CC + c + 1)
                        act.activation(yt[:, c, :], yt[:, c, :], ACT.Identity, bias=vec_at("beta", c),
                                       scale=vec_at("gamma", c)).then_inc(res_ok, 1)
                    act.sem_inc(nrm_ok, 1)

            @block.vector
            def _(dve):
                ch = [0]
                STEPS = 10

                def link(ins, b=None):
                    ch[0] += 1
                    ins.then_inc(dchain, 1)
                    dve.wait_ge(dchain, ch[0] if b is None else b * STEPS + ch[0])

                dve.sem_inc(pt_ok, 2)
                dve.sem_inc(at_ok, 1)
                dve.sem_inc(y_ok, 1)
                dve.memset(mean_w[:], 1.0 / C)
                dve.memset(eps[:], 1e-5)
                for j in range(2):
                    dve.memset(qx[j][D:D + 2, :], 1.0)
                dve.wait_ge(const_in, 8 * 16)
                dve.tensor_scalar(bq8[:], vecs[:, V0["bq"]:V0["bq"] + CC], SCALE0, None, ALU.mult)
                dve.tensor_scalar(bsp[:, 1:2], bsp[:, 0:1], -1.0, None, ALU.mult).then_inc(const_ok, 1)
                with dve.Fori(0, B) as b:
                    ch[0] = 0
                    dve.wait_ge(x_in, (b + 1) * 16)
                    dve.tensor_reduce(pooled[:], xraw[:], AX_X, ALU.add).then_inc(pool_ok, 1)
                    dve.wait_ge(se2_ps, b + 1)
                    dve.tensor_tensor(sez[:], ps_t[1][:, 0:CC], vecs[:, V0["bse2"]:V0["bse2"] + CC],
                                      ALU.add).then_inc(sez_ok, 1)
                    dve.wait_ge(see_ok, b + 1)
                    link(dve.tensor_scalar(sez[:], sez[:], 1.0, None, ALU.add), b)
                    dve.reciprocal(cw[:], sez[:]).then_inc(cw_ok, 1)
                    dve.wait_ge(sp_e, b + 1)
                    link(dve.tensor_scalar(gate[:], gate[:], 1.0, None, ALU.add), b)
                    link(dve.reciprocal(gate[:], gate[:]), b)
                    pixels = gate[:].rearrange("p (h w) -> p w h", h=H)
                    for i, (lo, hi) in enumerate(bins(H)):
                        last = dve.tensor_reduce(rows[:, i, :], pixels[:, :, lo:hi], AX_X, ALU.add)
                    link(last, b)
                    for first in (0, 1):
                        n = bins(H)[first][1] - bins(H)[first][0]
                        last = dve.tensor_scalar(rows[:, first::2, :], rows[:, first::2, :], 1.0 / n, None, ALU.mult)
                    link(last, b)
                    for i, (lo, hi) in enumerate(bins(W)):
                        last = dve.tensor_reduce(cells[:, :, i:i + 1], rows[:, :, lo:hi], AX_X, ALU.add)
                    link(last, b)
                    for first in (0, 1):
                        n = bins(W)[first][1] - bins(W)[first][0]
                        last = dve.tensor_scalar(cells[:, :, first::2], cells[:, :, first::2], 1.0 / n, 0.5,
                                                 ALU.mult, ALU.is_gt)
                    link(last, b)
                    for i, (lo, hi) in enumerate(spread(W)):
                        last = dve.tensor_copy(wide[:, :, lo:hi], cells[:, :, i:i + 1].broadcast_to([HEADS, G, hi - lo]))
                    link(last, b)
                    grid = mrow[:, 1, :].rearrange("p (h w) -> p h w", h=H)
                    for i, (lo, hi) in enumerate(spread(H)):
                        last = dve.tensor_copy(grid[:, lo:hi, :], wide[:, i:i + 1, :].broadcast_to([HEADS, hi - lo, W]))
                    link(last, b)
                    dve.tensor_scalar(mrow[:, 0, :], mrow[:, 1, :], -NEG, NEG, ALU.mult, ALU.add).then_inc(mask_ok, 1)
                    with dve.Fori(0, PAIRS) as p:
                        it = dve.snap(b * PAIRS + p)
                        dve.wait_ge(v_ps, it + 1)
                        dve.tensor_copy(vt[:].rearrange("p m n -> p (m n)"), ps_s[0][:]).then_inc(v_ok, 1)

                        def maxima(i):
                            dve.wait_ge(s_ps, it * TILES + i + 1)
                            dve.tensor_reduce(nmax[:, i:i + 1], ps_s[i % 2][:], AX_X, ALU.max,
                                              negate=True).then_inc(max_ok, 1)

                        def invert(i):
                            dve.wait_ge(exp_ok, it * TILES + i + 2)
                            dve.reciprocal(zinv[:, i:i + 1], zsum[:, i:i + 1]).then_inc(zinv_ok, 1)

                        def place(i):
                            j, g = divmod(i // 4, 2)
                            lanes = slice(D * j, D * j + D)
                            dve.wait_ge(zrow_ok, it * 4 + i // 4 + 1)
                            dst = attn[lanes, bass.ds(p, 1), g * HALF:(g + 1) * HALF].rearrange("p o n -> p (o n)")
                            link2(dve.tensor_tensor(dst, ps_o[lanes, :], zrow[lanes, :], ALU.mult), i)
                            dve.tensor_scalar(dst, dst, vecs[lanes, bass.ds(p + V0["bv"], 1)], None,
                                              ALU.add).then_inc(at_ok, 1)

                        def link2(ins, i):
                            ins.then_inc(place_ok, 1)
                            dve.wait_ge(place_ok, it * 4 + i // 4 + 1)

                        maxima(0)
                        for i in range(TILES):
                            if i + 1 < TILES:
                                maxima(i + 1)
                            invert(i)
                            if i % 4 == 0 and i:
                                place(i - 1)
                        place(TILES - 1)
                    for c in range(CC):
                        dve.wait_ge(ln_ps, b * (CC + 2) + c + 1)
                        dve.scalar_tensor_tensor(yt[:, c, :], ps_s[c % 2][:], vec_at("bo", c), xf[:, c, :],
                                                 ALU.add, ALU.add).then_inc(y_ok, 1)
                    dve.wait_ge(ln_ps, b * (CC + 2) + CC + 1)
                    for c in range(CC):
                        dve.tensor_tensor(yt[:, c, :], yt[:, c, :], ps_s[0][:], ALU.subtract).then_inc(cen_ok, 1)
                    dve.wait_ge(std_ok, b + 1)
                    link(dve.reciprocal(rstd[:], rstd[:]), b)
                    for c in range(CC):
                        dve.tensor_tensor(yt[:, c, :], yt[:, c, :], rstd[:], ALU.mult).then_inc(rstd_ok, 1)
                    assert ch[0] == STEPS, ch[0]


def layer1(nc, y, w_qkv, w1_d, w2_d, vec, bv_d, pe_d, out):
    with ExitStack() as ctx:
        def sb(name, shape):
            return ctx.enter_context(nc.sbuf_tensor(name, shape, F32))

        def ps(name, shape):
            return ctx.enter_context(nc.psum_tensor(name, shape, F32))

        def sem(name):
            return ctx.enter_context(nc.semaphore(name))

        w1 = sb("w1", [P, CC, C])
        w2 = sb("w2", [P, CC, C])
        vecs = sb("vecs1", [P, len(V1) * CC])
        bv = sb("bv1", [P, C])
        pos = sb("pos", [P, N])
        wpair = sb("wpair1", [P, CC, 2 * P])
        xin = sb("xin", [P, CC, N])
        qt = sb("qt", [QS1, N])
        kt = sb("kt", [QS1, N])
        vt = sb("vt1", [P, NT, P])
        vs = sb("vs", [P, 2, D])
        prob = sb("prob1", [P, 2, N])
        attn = sb("attn1", [P, CC, N])
        hid = sb("hid1", [P, CC, N])
        z = sb("z", [P, N])
        e = sb("e", [P, N])
        num = sb("num", [P, N])
        den = sb("den", [P, N])
        res = sb("res", [P, CC, N])
        nmax = sb("nmax1", [P, TILES])
        nms = sb("nms", [P, TILES])
        zsum = sb("zsum1", [P, TILES])
        zinv = sb("zinv1", [P, TILES])

        ps_s = [ps(f"ps1_s{i}", [P, N]) for i in range(2)]
        ps_o = ps("ps1_o", [P, N])
        ps_p = ps("ps1_p", [P, N])

        const_in = sem("const1_in")
        x_in = sem("x1_in")
        w_in = sem("w1_in")
        out_done = sem("out_done")
        qk_ps = sem("qk1_ps")
        v_ps = sem("v1_ps")
        qk_ok = sem("qk1_ok")
        v_ok = sem("v1_ok")
        s_ps = sem("s1_ps")
        max_ok = sem("max1_ok")
        nms_ok = sem("nms_ok")
        exp_ok = sem("exp1_ok")
        zinv_ok = sem("zinv1_ok")
        vs_ok = sem("vs_ok")
        o_ps = sem("o1_ps")
        at_ok = sem("at1_ok")
        h_ps = sem("h_ps")
        z_ok = sem("z_ok")
        zc_ok = sem("zc_ok")
        e_ok = sem("e_ok")
        mish_ok = sem("mish_ok")
        r_ps = sem("r_ps")
        res_ok = sem("res1_ok")
        mchain = sem("mchain")

        with nc.Block() as block:

            @block.sync
            def _(sp):
                for dst, src in ((w1, w1_d), (w2, w2_d), (vecs, vec), (pos, pe_d)):
                    sp.dma_start(dst[:], src).then_inc(const_in, 16)
                sp.dma_start(bv[:], bv_d.partition_broadcast(P)).then_inc(const_in, 16)
                sp.dma_start(wpair[:], w_qkv[0]).then_inc(w_in, 16)
                sp.sem_inc(out_done, 1)
                with sp.Fori(0, B) as b:
                    sp.wait_ge(res_ok, b * CC + 1)
                    sp.dma_start(xin[:], y[bass.ds(b, 1)].rearrange("o p c n -> (o p) c n")).then_inc(x_in, 16)
                    with sp.Fori(0, PAIRS) as p:
                        nxt_pair = sp.snap((p + 1) % PAIRS)
                        sp.wait_ge(out_done, b * CC * 16 + 1)
                        sp.wait_ge(v_ps, b * PAIRS + p + 1)
                        sp.dma_start(wpair[:], w_qkv[bass.ds(nxt_pair, 1)]
                                     .rearrange("o p c n -> (o p) c n")).then_inc(w_in, 16)
                    for c in range(CC):
                        sp.wait_ge(res_ok, b * CC + c + 2)
                        sp.dma_start(out[bass.ds(b, 1), c * P:(c + 1) * P, :].rearrange("o p n -> (o p) n"),
                                     res[:, c, :]).then_inc(out_done, 16)
                sp.wait_ge(out_done, B * CC * 16 + 1)
                sp.wait_ge(w_in, (B * PAIRS + 1) * 16)

            @block.tensor
            def _(pe):
                pe.wait_ge(const_in, 5 * 16)
                with pe.Fori(0, B) as b:
                    with pe.Fori(0, PAIRS) as p:
                        it = pe.snap(b * PAIRS + p)
                        pe.wait_ge(x_in, (b + 1) * 16)
                        pe.wait_ge(w_in, (it + 1) * 16)
                        for g in range(NH):
                            for c in range(CC):
                                mm = pe.matmul(ps_p[:, g * HALF:(g + 1) * HALF], wpair[:, c, 0:P],
                                               xin[:, c, g * HALF:(g + 1) * HALF], start=c == 0, stop=c == CC - 1)
                        mm.then_inc(qk_ps, 1)
                        pe.wait_ge(exp_ok, it * TILES + 1)
                        for m in range(NT):
                            for c in range(CC):
                                mm = pe.matmul(ps_s[0][:, m * P:(m + 1) * P], xin[:, c, m * P:(m + 1) * P],
                                               wpair[:, c, P:2 * P], start=c == 0, stop=c == CC - 1)
                        mm.then_inc(v_ps, 1)
                        pe.wait_ge(qk_ok, (it + 1) * 2)
                        pe.wait_ge(v_ok, it + 1)

                        def scores(i):
                            j, t = divmod(i, NT)
                            lanes = slice(DQ * j, DQ * j + DQ)
                            if i >= 2:
                                pe.wait_ge(exp_ok, it * TILES + i)
                            for g in range(NH):
                                mm = pe.matmul(ps_s[i % 2][:, g * HALF:(g + 1) * HALF],
                                               kt[lanes, t * P:(t + 1) * P], qt[lanes, g * HALF:(g + 1) * HALF],
                                               start=True, stop=True)
                            mm.then_inc(s_ps, 1)

                        def values(i):
                            j, t = divmod(i, NT)
                            lanes = slice(D * j, D * j + D)
                            if i == 0:
                                pe.wait_ge(at_ok, it + 1)
                            pe.wait_ge(vs_ok, it * TILES + i + 1)
                            for g in range(NH):
                                mm = pe.matmul(ps_o[lanes, g * HALF:(g + 1) * HALF], vs[:, i % 2, :],
                                               prob[:, i % 2, g * HALF:(g + 1) * HALF], start=t == 0, stop=t == NT - 1)
                            mm.then_inc(o_ps, 1)

                        scores(0)
                        for i in range(TILES):
                            if i + 1 < TILES:
                                scores(i + 1)
                            values(i)
                    pe.wait_ge(at_ok, (b + 1) * PAIRS + 1)
                    for o in range(CC):
                        if o >= 2:
                            pe.wait_ge(z_ok, b * CC + o - 1)
                        for g in range(NH):
                            for c in range(CC):
                                mm = pe.matmul(ps_s[o % 2][:, g * HALF:(g + 1) * HALF], w1[:, c, o * P:(o + 1) * P],
                                               attn[:, c, g * HALF:(g + 1) * HALF], start=c == 0, stop=c == CC - 1)
                        mm.then_inc(h_ps, 1)
                    pe.wait_ge(mish_ok, (b + 1) * CC)
                    for o in range(CC):
                        if o >= 2:
                            pe.wait_ge(res_ok, b * CC + o)
                        for g in range(NH):
                            for c in range(CC):
                                mm = pe.matmul(ps_s[o % 2][:, g * HALF:(g + 1) * HALF], w2[:, c, o * P:(o + 1) * P],
                                               hid[:, c, g * HALF:(g + 1) * HALF], start=c == 0, stop=c == CC - 1)
                        mm.then_inc(r_ps, 1)
                    pe.wait_ge(res_ok, (b + 1) * CC + 1)

            @block.scalar
            def _(act):
                act.sem_inc(exp_ok, 1)
                act.sem_inc(at_ok, 1)
                act.wait_ge(const_in, 5 * 16)
                with act.Fori(0, B) as b:
                    with act.Fori(0, PAIRS) as p:
                        it = act.snap(b * PAIRS + p)

                        def exps(i):
                            act.wait_ge(nms_ok, it * TILES + i + 1)
                            if i >= 2:
                                act.wait_ge(o_ps, it * TILES + i - 1)
                            act.activation(prob[:, i % 2, :], ps_s[i % 2][:], ACT.Exp, bias=nms[:, i:i + 1],
                                           scale=SCALE1, accum_out=zsum[:, i:i + 1]).then_inc(exp_ok, 1)

                        for i in range(TILES):
                            exps(i)
                        act.wait_ge(o_ps, (it + 1) * TILES)
                        act.activation(attn[:, bass.ds(p, 1), :].rearrange("p o n -> p (o n)"), ps_o[:],
                                       ACT.Identity).then_inc(at_ok, 1)
                    for c in range(CC):
                        act.wait_ge(h_ps, b * CC + c + 1)
                        if c:
                            act.wait_ge(mish_ok, b * CC + c)
                        act.activation(z[:], ps_s[c % 2][:], ACT.Identity,
                                       bias=vecs[:, V1["b1"] + c:V1["b1"] + c + 1]).then_inc(z_ok, 1)
                        act.wait_ge(zc_ok, b * CC + c + 1)
                        act.activation(e[:], e[:], ACT.Exp).then_inc(e_ok, 1)

            @block.vector
            def _(dve):
                dve.sem_inc(res_ok, 1)
                dve.wait_ge(const_in, 5 * 16)
                with dve.Fori(0, B) as b:
                    with dve.Fori(0, PAIRS) as p:
                        it = dve.snap(b * PAIRS + p)
                        dve.wait_ge(qk_ps, it + 1)
                        for dst, lanes in ((qt, slice(0, QS1)), (kt, slice(QS1, P))):
                            dve.scalar_tensor_tensor(dst[:], ps_p[lanes, :], vecs[lanes, bass.ds(p + V1["bqk"], 1)],
                                                     pos[lanes, :], ALU.add, ALU.add).then_inc(qk_ok, 1)
                        dve.wait_ge(v_ps, it + 1)
                        dve.tensor_tensor(vt[:], ps_s[0][:].rearrange("p (m n) -> p m n", m=NT),
                                          bv[:, bass.ds(p * P, P)].rearrange("p (o n) -> p o n", o=1)
                                          .broadcast_to([P, NT, P]), ALU.add).then_inc(v_ok, 1)

                        def maxima(i):
                            dve.wait_ge(s_ps, it * TILES + i + 1)
                            dve.tensor_reduce(nmax[:, i:i + 1], ps_s[i % 2][:], AX_X, ALU.max,
                                              negate=True).then_inc(max_ok, 1)
                            dve.wait_ge(max_ok, it * TILES + i + 1)
                            dve.tensor_scalar(nms[:, i:i + 1], nmax[:, i:i + 1], SCALE1, None,
                                              ALU.mult).then_inc(nms_ok, 1)

                        def weigh(i):
                            j, t = divmod(i, NT)
                            dve.wait_ge(exp_ok, it * TILES + i + 2)
                            dve.reciprocal(zinv[:, i:i + 1], zsum[:, i:i + 1]).then_inc(zinv_ok, 1)
                            dve.wait_ge(zinv_ok, it * TILES + i + 1)
                            if i >= 2:
                                dve.wait_ge(o_ps, it * TILES + i - 1)
                            dve.tensor_scalar(vs[:, i % 2, :], vt[:, t, D * j:D * j + D], zinv[:, i:i + 1], None,
                                              ALU.mult).then_inc(vs_ok, 1)

                        maxima(0)
                        for i in range(TILES):
                            if i + 1 < TILES:
                                maxima(i + 1)
                            weigh(i)
                    for c in range(CC):
                        def step(ins, k):
                            ins.then_inc(mchain, 1)
                            dve.wait_ge(mchain, (b * CC + c) * 4 + k)
                        dve.wait_ge(z_ok, b * CC + c + 1)
                        dve.tensor_scalar(e[:], z[:], MISH_TOP, None, ALU.min).then_inc(zc_ok, 1)
                        dve.wait_ge(e_ok, b * CC + c + 1)
                        step(dve.scalar_tensor_tensor(num[:], e[:], 2.0, e[:], ALU.add, ALU.mult), 1)
                        step(dve.tensor_scalar(den[:], num[:], 2.0, None, ALU.add), 2)
                        step(dve.reciprocal(den[:], den[:]), 3)
                        step(dve.tensor_tensor(num[:], num[:], den[:], ALU.mult), 4)
                        dve.tensor_tensor(hid[:, c, :], num[:], z[:], ALU.mult).then_inc(mish_ok, 1)
                    for c in range(CC):
                        dve.wait_ge(r_ps, b * CC + c + 1)
                        dve.scalar_tensor_tensor(res[:, c, :], ps_s[c % 2][:], vecs[:, V1["b2"] + c:V1["b2"] + c + 1],
                                                 xin[:, c, :], ALU.add, ALU.add).then_inc(res_ok, 1)


def build(nc, x, w0_qkv, w0_out, vec0, w_sp, b_sp, w_se1, b_se1, w_se2, ident, w1_qkv, w1, w2, vec1, bv1, pos, out):
    mask_d = nc.dram_tensor("mask_rows", (HEADS, 2, N), F32, kind="Internal").ap()
    y = nc.dram_tensor("layer0_out", (B, P, CC, N), F32, kind="Internal").ap()
    layer0(nc, x, w0_qkv, w0_out, vec0, w_sp, b_sp, w_se1, b_se1, w_se2, ident, mask_d, y)
    layer1(nc, y, w1_qkv, w1, w2, vec1, bv1, pos, out)


def kernel(**inputs):
    import numpy as np
    import concourse.bacc as bacc
    from concourse.bass_utils import run_bass_kernel_spmd

    def arr(name):
        return np.asarray(inputs[name])

    def turned(w):
        return np.ascontiguousarray(w.T.reshape(CC, P, w.shape[0]).transpose(1, 0, 2))

    def columns(v):
        return v.reshape(-1, P).T

    l0 = {k: arr(f"L0_conv_{k}") for k in ("Wq", "Wk", "Wv", "Wo", "Wsp", "Wse1", "Wse2", "bq", "bk", "bv", "bo",
                                            "bsp", "bse1", "bse2", "gamma", "beta")}
    l1 = {k: arr(f"L1_conv_{k}") for k in ("PE", "Wq", "Wk", "Wv", "W1", "W2", "bq", "bk", "bv", "b1", "b2")}

    def by_pair(*ws):
        parts = [turned(w).reshape(P, CC, PAIRS, -1).transpose(2, 0, 1, 3) for w in ws]
        return np.ascontiguousarray(np.concatenate(parts, axis=3))

    bqk = np.concatenate([l1["bq"].reshape(PAIRS, QS1), l1["bk"].reshape(PAIRS, QS1)], axis=1).T
    given = {
        "x": np.ascontiguousarray(arr("x").reshape(B, CC, P, N).transpose(0, 2, 1, 3)),
        "w0_qkv": by_pair(l0["Wq"], l0["Wk"], l0["Wv"]),
        "w0_out": turned(l0["Wo"]),
        "vec0": np.ascontiguousarray(np.concatenate([columns(l0[k]) for k in V0], axis=1)),
        "w_sp": turned(l0["Wsp"]),
        "b_sp": np.ascontiguousarray(l0["bsp"].reshape(HEADS, 1)),
        "w_se1": turned(l0["Wse1"]),
        "b_se1": np.ascontiguousarray(l0["bse1"].reshape(SE, 1)),
        "w_se2": np.ascontiguousarray(l0["Wse2"].T),
        "ident": np.eye(P, dtype=np.float32),
        "w1_qkv": by_pair(l1["Wq"], l1["Wk"], l1["Wv"]),
        "w1": turned(l1["W1"]),
        "w2": turned(l1["W2"]),
        "vec1": np.ascontiguousarray(np.concatenate([bqk, columns(l1["b1"]), columns(l1["b2"])], axis=1)),
        "bv1": np.ascontiguousarray(l1["bv"]),
        "pos": np.ascontiguousarray(np.concatenate([l1["PE"].reshape(DQ, N)] * (P // DQ), axis=0)),
    }
    nc = bacc.Bacc("TRN2", target_bir_lowering=False, num_devices=1)
    args = [nc.dram_tensor(f"in_{k}", v.shape, F32, kind="ExternalInput").ap() for k, v in given.items()]
    out = nc.dram_tensor("out_0", (B, C, N), F32, kind="ExternalOutput").ap()
    build(nc, *args, out)
    r = run_bass_kernel_spmd(nc, [{f"in_{k}": v for k, v in given.items()}], core_ids=[0])
    return r.results[0]["out_0"].reshape(B, C, H, W)
```

```python
from contextlib import ExitStack

import concourse.bass as bass
from concourse import mybir

F32 = mybir.dt.float32
F32R = mybir.dt.float32r
ALU = mybir.AluOpType
ACT = mybir.ActivationFunctionType
AX_X = mybir.AxisListType.X

P = 128
B, C, H, W = 8, 512, 32, 32
N = H * W
HALF = 512
NH = N // HALF
CC = C // P
HEADS = 8
PAIRS = HEADS // 2
D = C // HEADS
NT = N // P
TILES = 2 * NT
GT = TILES // NH
SE = C // 16
G = 7
NEG = -1000000000.0
NEG_HI = float(round(NEG / 2 ** 18) * 2 ** 18)
NEG_LO = NEG - NEG_HI
DQ = 32
QS1 = 2 * DQ
SCALE0 = D ** -0.5
SCALE1 = 1.0 / float(DQ) ** 0.5
FIRST = 0
MISH_TOP = 20.0

V0 = {name: i * CC for i, name in enumerate(["bq", "bk", "bv", "bo", "bse2", "gamma", "beta"])}
V1 = {name: i * CC for i, name in enumerate(["bqk", "b1", "b2"])}


def bins(n):
    return [(i * n // G, -(-(i + 1) * n // G)) for i in range(G)]


def spread(n):
    cell = [i * G // n for i in range(n)]
    return [(cell.index(g), n - cell[::-1].index(g)) for g in range(G)]


def layer0(nc, x, w_qkv, w_out, vec, w_sp, b_sp, w_se1, b_se1, w_se2, ident_d, mask_d, y):
    with ExitStack() as ctx:
        def sb(name, shape, dt=F32):
            return ctx.enter_context(nc.sbuf_tensor(name, shape, dt))

        def ps(name, shape):
            return ctx.enter_context(nc.psum_tensor(name, shape, F32))

        def sem(name):
            return ctx.enter_context(nc.semaphore(name))

        ident = sb("ident0", [P, P])
        mean_w = sb("mean_w", [P, P])
        wo = sb("wo", [P, CC, C])
        vecs = sb("vecs0", [P, len(V0) * CC])
        bq8 = sb("bq8", [P, CC])
        eps = sb("eps", [P, 1])
        wsp = sb("wsp", [P, CC, HEADS])
        bsp = sb("bsp", [HEADS, 2])
        wse1 = sb("wse1", [P, CC, SE])
        bse1 = sb("bse1", [SE, 1])
        wse2 = sb("wse2", [SE, C])
        wpair = sb("wpair0", [P, CC, 3 * P])
        xraw = sb("xraw", [P, CC, N])
        xf = sb("xf", [P, CC, N])
        attn = sb("attn0", [P, CC, N])
        yt = sb("yt", [P, CC, N])
        rstd = sb("rstd", [P, N])
        gate = sb("gate", [HEADS, N])
        rows = sb("rows", [HEADS, G, W])
        cells = sb("cells", [HEADS, G, G])
        wide = sb("wide", [HEADS, G, W])
        mrow = sb("mrow", [HEADS, 3, N])
        pooled = sb("pooled", [P, CC])
        hid = sb("hid", [SE, 1])
        sez = sb("sez", [P, CC])
        cw = sb("cw", [P, CC])
        full = sb("full", [P, N])
        high = sb("high", [P, N], F32R)
        low = sb("low", [P, N], F32R)
        q1 = [sb(f"q1_{j}", [P, N], F32R) for j in range(2)]
        k1 = [sb(f"k1_{j}", [P, N], F32R) for j in range(2)]
        q2 = [sb(f"q2_{j}", [D + 4, N], F32R) for j in range(2)]
        k2 = [sb(f"k2_{j}", [D + 4, N], F32R) for j in range(2)]
        vt = sb("vt0", [P, NT, P])
        prob = sb("prob", [P, 2, N])
        pt = sb("pt", [P, 2, NT, HALF])
        nmax = sb("nmax0", [P, TILES])
        zsum = sb("zsum0", [P, TILES])
        zinv = sb("zinv0", [P, TILES])
        zrow = sb("zrow", [P, HALF])

        ps_s = [ps(f"ps_s{i}", [P, N]) for i in range(2)]
        ps_t = ps("ps_t", [P, N])
        ps_o = ps("ps_o", [P, HALF])
        ps_z = ps("ps_z", [P, HALF])

        const_in = sem("const_in")
        const_ok = sem("const_ok")
        x_in = sem("x_in")
        w_in = sem("w_in")
        mask_out = sem("mask_out")
        mask_in = sem("mask_in")
        q_in, k_in = sem("q_in"), sem("k_in")
        y_out = sem("y_out")
        sp_ps = sem("sp_ps")
        sp_e = sem("sp_e")
        mask_ok = sem("mask_ok")
        pool_ok = sem("pool_ok")
        se1_ps, hid_ok, se2_ps, sez_ok, see_ok = (sem(n) for n in ("se1_ps", "hid_ok", "se2_ps", "sez_ok", "see_ok"))
        cw_ok = sem("cw_ok")
        xf_ok = sem("xf_ok")
        q_ps, k_ps, v_ps = sem("q_ps"), sem("k_ps"), sem("v_ps")
        full_ok = sem("full_ok")
        high_ok = sem("high_ok")
        low_ok = sem("low_ok")
        v_ok = sem("v_ok")
        s_ps = sem("s_ps")
        max_ok = sem("max_ok")
        exp_ok = sem("exp_ok")
        t_ps = sem("t_ps")
        pt_a, pt_d = sem("pt_a"), sem("pt_d")
        zinv_ok = sem("zinv_ok")
        o_ps = sem("o_ps")
        zrow_ok = sem("zrow_ok")
        mul_ok = sem("mul_ok")
        at_ok = sem("at_ok")
        wo_ps = sem("wo_ps")
        y_ok = sem("y_ok")
        mean_ps, var_ps = sem("mean_ps"), sem("var_ps")
        cen_ok, sq_ok, std_ok, inv_ok, nrm_ok, res_ok = (
            sem(n) for n in ("cen_ok", "sq_ok", "std_ok", "inv_ok", "nrm_ok", "res_ok"))
        dchain = sem("dchain0")
        COPIES = 6 * 16

        def vec_at(name, c):
            return vecs[:, V0[name] + c:V0[name] + c + 1]

        def halves(t, g):
            return t[:, g * HALF:(g + 1) * HALF]

        with nc.Block() as block:

            @block.sync
            def _(sp):
                for dst, src in ((ident, ident_d), (wo, w_out), (vecs, vec), (wsp, w_sp), (bsp[:, 0:1], b_sp),
                                 (wse1, w_se1), (bse1, b_se1), (wse2, w_se2)):
                    sp.dma_start(dst[:] if dst is not bsp else dst, src).then_inc(const_in, 16)
                sp.dma_start(xraw[:], x[0]).then_inc(x_in, 16)
                sp.dma_start(wpair[:], w_qkv[0]).then_inc(w_in, 16)
                sp.wait_ge(const_ok, 1)

                def gates(k, nxt):
                    sp.wait_ge(mask_ok, k + 1)
                    sp.dma_start(mask_d[:, 0:3, :], mrow[:]).then_inc(mask_out, 16)
                    sp.dma_start(mask_d[:, 3:4, :], mrow[:, 2:3, :]).then_inc(mask_out, 16)
                    sp.wait_ge(xf_ok, k + 1)
                    sp.dma_start(xraw[:], x[nxt].rearrange("o p c n -> (o p) c n")).then_inc(x_in, 16)
                    sp.wait_ge(mask_out, (k + 1) * 32)

                def project(k, p, nxt):
                    sp.wait_ge(low_ok, k * 2 + 1)
                    for j in range(2):
                        own = slice(D * j, D * j + D)
                        sp.dma_start(q1[j][0:D, :].bitcast(F32), high[own, :].bitcast(F32)).then_inc(q_in, 16)
                        sp.dma_start(q1[j][D:P, :].bitcast(F32), low[own, :].bitcast(F32)).then_inc(q_in, 16)
                        sp.dma_start(q2[j][0:D, :].bitcast(F32), high[own, :].bitcast(F32)).then_inc(q_in, 16)
                    for j in range(2):
                        one = mask_d[bass.ds(p * 2 + j, 1)].rearrange("o r n -> (o r) n")
                        sp.dma_start(q2[j][D:D + 2, :].bitcast(F32), one[0:2, :]).then_inc(mask_in, 16)
                        sp.dma_start(k2[j][D:D + 2, :].bitcast(F32), one[2:4, :]).then_inc(mask_in, 16)
                        sp.dma_start(k2[j][D + 2:D + 4, :].bitcast(F32), one[0:2, :]).then_inc(mask_in, 16)
                    sp.wait_ge(low_ok, k * 2 + 2)
                    for j in range(2):
                        own = slice(D * j, D * j + D)
                        sp.dma_start(k1[j][0:D, :].bitcast(F32), high[own, :].bitcast(F32)).then_inc(k_in, 16)
                        sp.dma_start(k1[j][D:P, :].bitcast(F32), high[own, :].bitcast(F32)).then_inc(k_in, 16)
                        sp.dma_start(k2[j][0:D, :].bitcast(F32), low[own, :].bitcast(F32)).then_inc(k_in, 16)
                    sp.wait_ge(v_ps, k + 1)
                    sp.dma_start(wpair[:], w_qkv[nxt].rearrange("o p c n -> (o p) c n")).then_inc(w_in, 16)

                gates(0, slice(1, 2))
                project(0, 0, slice(1, 2))
                with sp.Fori(0, B) as b:
                    ahead = sp.snap((b + 2) % B)
                    with sp.Fori(0, PAIRS - 1) as p:
                        nxt = sp.snap((p + 2) % PAIRS)
                        project(sp.snap(b * PAIRS + p + 1), p + 1, bass.ds(nxt, 1))
                    gates(sp.snap(b + 1), bass.ds(ahead, 1))
                    project(sp.snap(b * PAIRS + PAIRS), 0, slice(1, 2))
                sp.wait_ge(y_out, B * CC * 16 + 1)
                sp.wait_ge(x_in, (B + 2) * 16)
                sp.wait_ge(w_in, (B * PAIRS + 2) * 16)
                sp.wait_ge(mask_in, (B * PAIRS + 1) * COPIES)
                sp.wait_ge(q_in, (B * PAIRS + 1) * COPIES)
                sp.wait_ge(k_in, (B * PAIRS + 1) * COPIES)

            @block.tensor
            def _(pe):
                def spatial(k):
                    pe.wait_ge(x_in, (k + 1) * 16)
                    for g in range(NH):
                        for c in range(CC):
                            mm = pe.matmul(halves(ps_s[0][0:HEADS], g), wsp[:, c, :], halves(xraw[:, c, :], g),
                                           start=c == 0, stop=c == CC - 1)
                    mm.then_inc(sp_ps, 1)

                def squeeze(k):
                    pe.wait_ge(pool_ok, k + 1)
                    for c in range(CC):
                        mm = pe.matmul(ps_s[1][0:SE, 0:1], wse1[:, c, :], pooled[:, c:c + 1],
                                       start=c == 0, stop=c == CC - 1)
                    mm.then_inc(se1_ps, 1)

                def excite(k):
                    pe.wait_ge(hid_ok, k + 1)
                    for c in range(CC):
                        mm = pe.matmul(ps_s[1][:, HALF + c:HALF + c + 1], wse2[:, c * P:(c + 1) * P], hid[:],
                                       start=True, stop=True)
                    mm.then_inc(se2_ps, 1)

                def chunk_product(dst, w, src, done):
                    for g in range(NH):
                        for c in range(CC):
                            mm = pe.matmul(halves(dst, g), w(c), halves(src(c), g), start=c == 0, stop=c == CC - 1)
                    mm.then_inc(done, 1)

                def queries(k):
                    pe.wait_ge(w_in, (k + 1) * 16)
                    chunk_product(ps_s[0], lambda c: wpair[:, c, 0:P], lambda c: xf[:, c, :], q_ps)

                def keys(k):
                    chunk_product(ps_s[1], lambda c: wpair[:, c, P:2 * P], lambda c: xf[:, c, :], k_ps)

                def pair_values(k):
                    pe.wait_ge(full_ok, k * 2 + 1)
                    for m in range(NT):
                        for c in range(CC):
                            mm = pe.matmul(ps_s[0][:, m * P:(m + 1) * P], xf[:, c, m * P:(m + 1) * P],
                                           wpair[:, c, 2 * P:3 * P], start=c == 0, stop=c == CC - 1)
                    mm.then_inc(v_ps, 1)

                def attend(it, first, rest):
                    def scores(i):
                        j, t = i % 2, i // 2
                        if i == 0:
                            pe.wait_ge(v_ok, it + 1)
                        if i >= 2:
                            pe.wait_ge(exp_ok, it * TILES + i - 1)
                        for g in range(NH):
                            pe.matmul(halves(ps_s[j], g), q1[j][:, t * P:(t + 1) * P], halves(k1[j], g),
                                      start=True, stop=False)
                            mm = pe.matmul(halves(ps_s[j], g), q2[j][:, t * P:(t + 1) * P], halves(k2[j], g),
                                           start=False, stop=True)
                        mm.then_inc(s_ps, 1)

                    def turn(i):
                        pe.wait_ge(exp_ok, it * TILES + i + 1)
                        for h, copied in ((0, pt_a), (1, pt_d)):
                            if i:
                                pe.wait_ge(copied, it * TILES + i)
                            for m in range(4 * h, 4 * h + 4):
                                mm = pe.transpose(ps_t[:, m * P:(m + 1) * P], prob[:, i % 2, m * P:(m + 1) * P],
                                                  ident[:])
                            mm.then_inc(t_ps, 1)

                    def weigh(g):
                        last = GT * g + GT - 1
                        pe.wait_ge(pt_a, it * TILES + last + 1)
                        pe.wait_ge(pt_d, it * TILES + last + 1)
                        if g:
                            pe.wait_ge(at_ok, it * NH + g)
                        for m in range(NT):
                            for j in range(2):
                                own = slice(D * j, D * j + D)
                                pe.matmul(ps_o[own, :], vt[:, m, own], pt[:, j, m, :],
                                          start=m == 0, stop=m == NT - 1)
                        pe.wait_ge(zinv_ok, it * TILES + last + 1)
                        for t in range(GT // 2):
                            for j in range(2):
                                i = GT * g + 2 * t + j
                                mm = pe.matmul(ps_z[D * j:D * j + D, t * P:(t + 1) * P],
                                               zinv[:, i:i + 1].broadcast_to([P, D]), ident[:],
                                               start=True, stop=True)
                        mm.then_inc(o_ps, 1)

                    pe.wait_ge(q_in, (it + 1) * COPIES)
                    pe.wait_ge(k_in, (it + 1) * COPIES)
                    pe.wait_ge(mask_in, (it + 1) * COPIES)
                    scores(0)
                    scores(1)
                    for i in range(TILES - 1):
                        if i >= 1 and i != GT:
                            scores(i + 1)
                        turn(i)
                        if i == GT - 1:
                            scores(i + 2)
                            weigh(0)
                    pe.wait_ge(exp_ok, it * TILES + TILES - 1)
                    first()
                    turn(TILES - 1)
                    rest()
                    weigh(1)

                pe.wait_ge(const_in, 8 * 16)
                pe.wait_ge(const_ok, 1)
                spatial(0)
                squeeze(0)
                excite(0)
                pe.wait_ge(xf_ok, 1)
                pe.wait_ge(sp_e, 1)
                queries(0)
                keys(0)
                pair_values(0)
                with pe.Fori(0, B) as b:
                    with pe.Fori(0, PAIRS - 1) as p:
                        it = pe.snap(b * PAIRS + p)
                        attend(it, lambda: queries(it + 1), lambda: keys(it + 1))
                        pair_values(it + 1)
                    it = pe.snap(b * PAIRS + PAIRS - 1)
                    attend(it, lambda: spatial(b + 1), lambda: squeeze(b + 1))
                    excite(b + 1)
                    pe.wait_ge(sp_e, b + 2)
                    pe.wait_ge(at_ok, (b + 1) * NH * PAIRS)
                    for o in range(CC):
                        if o == 1:
                            pe.wait_ge(sez_ok, b + 2)
                        if o >= 2:
                            pe.wait_ge(y_ok, b * CC + o - 1)
                        chunk_product(ps_s[o % 2], lambda c: wo[:, c, o * P:(o + 1) * P],
                                      lambda c: attn[:, c, :], wo_ps)
                    pe.wait_ge(y_ok, (b + 1) * CC)
                    chunk_product(ps_t, lambda c: mean_w[:], lambda c: yt[:, c, :], mean_ps)
                    pe.wait_ge(xf_ok, b + 2)
                    queries(it + 1)
                    keys(it + 1)
                    pe.wait_ge(sq_ok, (b + 1) * CC)
                    chunk_product(ps_t, lambda c: mean_w[:], lambda c: attn[:, c, :], var_ps)
                    pair_values(it + 1)

            @block.scalar
            def _(act):
                def spatial(k):
                    act.wait_ge(sp_ps, k + 1)
                    act.activation(gate[:], ps_s[0][0:HEADS, :], ACT.Exp, bias=bsp[:, 1:2],
                                   scale=-1.0).then_inc(sp_e, 1)

                def squeeze(k):
                    act.wait_ge(se1_ps, k + 1)
                    act.activation(hid[:], ps_s[1][0:SE, 0:1], ACT.Relu, bias=bse1[:],
                                   scale=1.0 / N).then_inc(hid_ok, 1)

                def excite(k):
                    act.wait_ge(sez_ok, k + 1)
                    act.activation(sez[:], sez[:], ACT.Exp, scale=-1.0).then_inc(see_ok, 1)

                def gated(k):
                    act.wait_ge(cw_ok, k + 1)
                    for c in range(CC):
                        last = act.activation(xf[:, c, :], xraw[:, c, :], ACT.Identity, scale=cw[:, c:c + 1])
                    last.then_inc(xf_ok, 1)

                def queries(k, p):
                    act.wait_ge(q_ps, k + 1)
                    if k is not FIRST:
                        act.wait_ge(low_ok, k * 2)
                    act.activation(full[:], ps_s[0][:], ACT.Identity, bias=bq8[:, bass.ds(p, 1)],
                                   scale=SCALE0).then_inc(full_ok, 1)

                def keys(k, p):
                    act.wait_ge(k_ps, k + 1)
                    act.wait_ge(low_ok, k * 2 + 1)
                    act.activation(full[:], ps_s[1][:], ACT.Identity,
                                   bias=vecs[:, bass.ds(p + V0["bk"], 1)]).then_inc(full_ok, 1)

                def attend(it, steps):
                    def exps(i):
                        act.wait_ge(max_ok, it * TILES + i + 1)
                        if i >= 2:
                            act.wait_ge(t_ps, (it * TILES + i) * 2 - 2)
                        act.activation(prob[:, i % 2, :], ps_s[i % 2][:], ACT.Exp, bias=nmax[:, i:i + 1],
                                       accum_out=zsum[:, i:i + 1]).then_inc(exp_ok, 1)

                    def copy_t(i):
                        act.wait_ge(t_ps, (it * TILES + i) * 2 + 1)
                        q = i // 2 % 4
                        act.activation(pt[:, i % 2, 0:4, q * P:(q + 1) * P],
                                       ps_t[:, 0:HALF].rearrange("p (m n) -> p m n", m=4),
                                       ACT.Identity).then_inc(pt_a, 1)

                    def copy_z(g):
                        act.wait_ge(o_ps, it * NH + g + 1)
                        if g:
                            act.wait_ge(mul_ok, it * NH + g)
                        act.activation(zrow[:], ps_z[:], ACT.Identity).then_inc(zrow_ok, 1)

                    exps(0)
                    for i in range(TILES - 1):
                        exps(i + 1)
                        copy_t(i)
                        if i == GT:
                            copy_z(0)
                    steps[0]()
                    copy_t(TILES - 1)
                    steps[1]()
                    copy_z(1)

                act.sem_inc(y_out, 1)
                act.wait_ge(const_in, 8 * 16)
                act.wait_ge(const_ok, 1)
                spatial(0)
                squeeze(0)
                excite(0)
                gated(0)
                queries(FIRST, 0)
                keys(FIRST, 0)
                with act.Fori(0, B) as b:
                    with act.Fori(0, PAIRS - 1) as p:
                        it = act.snap(b * PAIRS + p)
                        attend(it, [lambda: queries(it + 1, p + 1), lambda: keys(it + 1, p + 1)])
                    it = act.snap(b * PAIRS + PAIRS - 1)
                    attend(it, [lambda: spatial(b + 1), lambda: squeeze(b + 1)])
                    excite(b + 1)
                    act.wait_ge(y_ok, (b + 1) * CC)
                    gated(b + 1)
                    for c in range(CC):
                        act.wait_ge(cen_ok, b * CC + c + 1)
                        act.activation(attn[:, c, :], yt[:, c, :], ACT.Square).then_inc(sq_ok, 1)
                    queries(it + 1, 0)
                    keys(it + 1, 0)
                    act.wait_ge(var_ps, b + 1)
                    act.activation(rstd[:], ps_t[:], ACT.Sqrt, bias=eps[:]).then_inc(std_ok, 1)
                    for c in range(CC):
                        act.wait_ge(nrm_ok, b * CC + c + 1)
                        act.activation(yt[:, c, :], yt[:, c, :], ACT.Identity, bias=vec_at("beta", c),
                                       scale=vec_at("gamma", c)).then_inc(res_ok, 1)
                    for c in range(CC):
                        act.wait_ge(res_ok, b * CC + c + 1)
                        act.dma_start(y[bass.ds(b, 1), :, c, :].rearrange("o p n -> (o p) n"),
                                      yt[:, c, :]).then_inc(y_out, 16)

            @block.vector
            def _(dve):
                ch = [0]
                STEPS = 8

                def link(ins, k):
                    ch[0] += 1
                    ins.then_inc(dchain, 1)
                    dve.wait_ge(dchain, k * STEPS + ch[0])

                def pool(k):
                    dve.wait_ge(x_in, (k + 1) * 16)
                    dve.tensor_reduce(pooled[:], xraw[:], AX_X, ALU.add).then_inc(pool_ok, 1)

                def excite(k):
                    dve.wait_ge(se2_ps, k + 1)
                    dve.tensor_tensor(sez[:], ps_s[1][:, HALF:HALF + CC], vecs[:, V0["bse2"]:V0["bse2"] + CC],
                                      ALU.add).then_inc(sez_ok, 1)
                    dve.wait_ge(see_ok, k + 1)
                    link(dve.tensor_scalar(sez[:], sez[:], 1.0, None, ALU.add), k)
                    dve.reciprocal(cw[:], sez[:]).then_inc(cw_ok, 1)

                def mask(k):
                    dve.wait_ge(sp_e, k + 1)
                    link(dve.tensor_scalar(gate[:], gate[:], 1.0, None, ALU.add), k)
                    link(dve.reciprocal(gate[:], gate[:]), k)
                    pixels = gate[:].rearrange("p (h w) -> p w h", h=H)
                    for i, (lo, hi) in enumerate(bins(H)):
                        last = dve.tensor_reduce(rows[:, i, :], pixels[:, :, lo:hi], AX_X, ALU.add)
                    link(last, k)
                    for first in (0, 1):
                        n = bins(H)[first][1] - bins(H)[first][0]
                        last = dve.tensor_scalar(rows[:, first::2, :], rows[:, first::2, :], 1.0 / n, None, ALU.mult)
                    link(last, k)
                    for i, (lo, hi) in enumerate(bins(W)):
                        last = dve.tensor_reduce(cells[:, :, i:i + 1], rows[:, :, lo:hi], AX_X, ALU.add)
                    link(last, k)
                    for first in (0, 1):
                        n = bins(W)[first][1] - bins(W)[first][0]
                        last = dve.tensor_scalar(cells[:, :, first::2], cells[:, :, first::2], 1.0 / n, 0.5,
                                                 ALU.mult, ALU.is_gt)
                    link(last, k)
                    for lo, hi, i in ((*s, i) for i, s in enumerate(spread(W))):
                        last = dve.tensor_copy(wide[:, :, lo:hi], cells[:, :, i:i + 1].broadcast_to([HEADS, G, hi - lo]))
                    link(last, k)
                    for r, (scale, bias) in enumerate(((-NEG_HI, NEG_HI), (-NEG_LO, NEG_LO), (1.0, 0.0))):
                        grid = mrow[:, r, :].rearrange("p (h w) -> p h w", h=H)
                        for i, (lo, hi) in enumerate(spread(H)):
                            last = dve.tensor_scalar(grid[:, lo:hi, :],
                                                     wide[:, i:i + 1, :].broadcast_to([HEADS, hi - lo, W]),
                                                     scale, bias, ALU.mult, ALU.add)
                    last.then_inc(mask_ok, 1)

                def split(n, last_in):
                    dve.wait_ge(full_ok, n)
                    if last_in is not None:
                        dve.wait_ge(*last_in)
                    dve.tensor_copy(high[:], full[:]).then_inc(high_ok, 1)
                    dve.wait_ge(high_ok, n)
                    dve.tensor_tensor(low[:], full[:], high[:].bitcast(F32), ALU.subtract).then_inc(low_ok, 1)

                def queries(k):
                    split(k * 2 + 1, (k_in, k * COPIES) if k is not FIRST else None)

                def keys(k):
                    split(k * 2 + 2, (q_in, (k + 1) * COPIES))

                def pair_values(k):
                    dve.wait_ge(v_ps, k + 1)
                    dve.tensor_copy(vt[:].rearrange("p m n -> p (m n)"), ps_s[0][:]).then_inc(v_ok, 1)

                def attend(it, p, steps):
                    def maxima(i):
                        dve.wait_ge(s_ps, it * TILES + i + 1)
                        dve.tensor_reduce(nmax[:, i:i + 1], ps_s[i % 2][:], AX_X, ALU.max,
                                          negate=True).then_inc(max_ok, 1)

                    def copy_t(i):
                        q = i // 2 % 4
                        dve.wait_ge(t_ps, (it * TILES + i) * 2 + 2)
                        dve.tensor_copy(pt[:, i % 2, 4:8, q * P:(q + 1) * P],
                                        ps_t[:, HALF:N].rearrange("p (m n) -> p m n", m=4)).then_inc(pt_d, 1)
                        dve.reciprocal(zinv[:, i:i + 1], zsum[:, i:i + 1]).then_inc(zinv_ok, 1)

                    def place(g):
                        dve.wait_ge(zrow_ok, it * NH + g + 1)
                        dst = attn[:, bass.ds(p, 1), g * HALF:(g + 1) * HALF].rearrange("p o n -> p (o n)")
                        dve.tensor_tensor(dst, ps_o[:], zrow[:], ALU.mult).then_inc(mul_ok, 1)
                        dve.wait_ge(mul_ok, it * NH + g + 1)
                        dve.tensor_scalar(dst, dst, vecs[:, bass.ds(p + V0["bv"], 1)], None,
                                          ALU.add).then_inc(at_ok, 1)

                    maxima(0)
                    for i in range(TILES - 1):
                        maxima(i + 1)
                        copy_t(i)
                        if i == GT:
                            place(0)
                    steps[0]()
                    copy_t(TILES - 1)
                    steps[1]()
                    place(1)

                dve.memset(mean_w[:], 1.0 / C)
                dve.memset(eps[:], 1e-5)
                for j in range(2):
                    dve.memset(q2[j][D:D + 4, :].bitcast(F32), 1.0)
                dve.wait_ge(const_in, 8 * 16)
                dve.tensor_scalar(bq8[:], vecs[:, V0["bq"]:V0["bq"] + CC], SCALE0, None, ALU.mult)
                dve.tensor_scalar(bsp[:, 1:2], bsp[:, 0:1], -1.0, None, ALU.mult).then_inc(const_ok, 1)
                pool(0)
                excite(0)
                mask(0)
                queries(FIRST)
                keys(FIRST)
                pair_values(0)
                with dve.Fori(0, B) as b:
                    with dve.Fori(0, PAIRS - 1) as p:
                        it = dve.snap(b * PAIRS + p)
                        attend(it, p, [lambda: queries(it + 1), lambda: keys(it + 1)])
                        pair_values(it + 1)
                    it = dve.snap(b * PAIRS + PAIRS - 1)
                    attend(it, PAIRS - 1, [lambda: pool(b + 1), lambda: None])
                    ch[0] = 0
                    excite(b + 1)
                    mask(b + 1)
                    assert ch[0] == STEPS, ch[0]
                    for c in range(CC):
                        dve.wait_ge(wo_ps, b * CC + c + 1)
                        if c == 0:
                            dve.wait_ge(y_out, b * CC * 16 + 1)
                        dve.scalar_tensor_tensor(yt[:, c, :], ps_s[c % 2][:], vec_at("bo", c), xf[:, c, :],
                                                 ALU.add, ALU.add).then_inc(y_ok, 1)
                    dve.wait_ge(mean_ps, b + 1)
                    for c in range(CC):
                        dve.tensor_tensor(yt[:, c, :], yt[:, c, :], ps_t[:], ALU.subtract).then_inc(cen_ok, 1)
                    queries(it + 1)
                    keys(it + 1)
                    dve.wait_ge(std_ok, b + 1)
                    dve.reciprocal(rstd[:], rstd[:]).then_inc(inv_ok, 1)
                    dve.wait_ge(inv_ok, b + 1)
                    for c in range(CC):
                        dve.tensor_tensor(yt[:, c, :], yt[:, c, :], rstd[:], ALU.mult).then_inc(nrm_ok, 1)
                    pair_values(it + 1)


def layer1(nc, y, w_qkv, w1_d, w2_d, vec, bv_d, pe_d, out):
    with ExitStack() as ctx:
        def sb(name, shape, dt=F32):
            return ctx.enter_context(nc.sbuf_tensor(name, shape, dt))

        def ps(name, shape):
            return ctx.enter_context(nc.psum_tensor(name, shape, F32))

        def sem(name):
            return ctx.enter_context(nc.semaphore(name))

        w1 = sb("w1", [P, CC, C])
        w2 = sb("w2", [P, CC, C])
        vecs = sb("vecs1", [P, len(V1) * CC])
        bv = sb("bv1", [P, C])
        pos = sb("pos", [P, N])
        wpair = [sb(f"wpair1_{u}", [P, CC, 2 * P]) for u in range(2)]
        xin = sb("xin", [P, CC, N])
        full = sb("full1", [P, N])
        high = sb("high1", [P, N], F32R)
        low = sb("low1", [P, N], F32R)
        ks = [[sb(f"ks{u}_{j}", [P, N], F32R) for j in range(2)] for u in range(2)]
        qs = [[sb(f"qs{u}_{j}", [P, N], F32R) for j in range(2)] for u in range(2)]
        vt = [sb(f"vt1_{u}", [P, NT, P]) for u in range(2)]
        vs = sb("vs", [P, 2, 2, D])
        prob = sb("prob1", [P, 2, 2, N])
        attn = sb("attn1", [P, CC, N])
        hid = sb("hid1", [P, CC, N])
        z = sb("z", [P, N])
        e = sb("e", [P, N])
        num = sb("num", [P, N])
        inv = sb("inv", [P, N])
        two = sb("two", [P, 1])
        res = sb("res", [P, CC, N])
        nmax = sb("nmax1", [P, TILES])
        nms = sb("nms", [P, TILES])
        zsum = sb("zsum1", [P, TILES])
        zinv = sb("zinv1", [P, TILES])

        ps_s = [ps(f"ps1_s{i}", [P, N]) for i in range(2)]
        ps_o = ps("ps1_o", [P, N])
        ps_p = ps("ps1_p", [P, N])

        const_in = sem("const1_in")
        x_in = sem("x1_in")
        r_in = sem("r1_in")
        w_in = [sem("w1_in0"), sem("w1_in1")]
        op_in = sem("op_in")
        out_done = sem("out_done")
        qk_ps = sem("qk1_ps")
        v_ps = sem("v1_ps")
        full_ok, high_ok, low_ok = sem("full1_ok"), sem("high1_ok"), sem("low1_ok")
        v_ok = sem("v1_ok")
        s_ps = sem("s1_ps")
        max_ok = sem("max1_ok")
        nms_ok = sem("nms_ok")
        exp_ok = sem("exp1_ok")
        zinv_ok = sem("zinv1_ok")
        vs_ok = sem("vs_ok")
        o_ps = sem("o1_ps")
        at_ok = sem("at1_ok")
        h_ps = sem("h_ps")
        z_ok, zc_ok, e_ok, num_ok, ln_ok, inv_ok = (
            sem(n) for n in ("z_ok", "zc_ok", "e_ok", "num_ok", "ln_ok", "inv1_ok"))
        mish_ok = sem("mish_ok")
        r_ps = sem("r_ps")
        res_ok = sem("res1_ok")
        mchain = sem("mchain")
        MOVES = 16 * 16
        QK_STEP, V_STEP = 0, 4
        V_TILES = ([0, 1, 2], [3, 4, 5], [6, 7])

        def halves(t, g):
            return t[:, g * HALF:(g + 1) * HALF]

        with nc.Block() as block:

            @block.sync
            def _(sp):
                for dst, src in ((w1, w1_d), (w2, w2_d), (vecs, vec), (pos, pe_d)):
                    sp.dma_start(dst[:], src).then_inc(const_in, 16)
                sp.dma_start(bv[:], bv_d.partition_broadcast(P)).then_inc(const_in, 16)
                for u in range(2):
                    sp.dma_start(wpair[u][:], w_qkv[u]).then_inc(w_in[u], 16)
                sp.dma_start(xin[:], y[0]).then_inc(x_in, 16)

                def operands(k, u):
                    sp.wait_ge(low_ok, k + 1)
                    for j in range(2):
                        q = slice(DQ * j, DQ * j + DQ)
                        kk = slice(QS1 + DQ * j, QS1 + DQ * j + DQ)
                        for quad, (q_part, k_part) in enumerate(((high, high), (high, low), (low, high), (low, low))):
                            own = slice(quad * DQ, quad * DQ + DQ)
                            sp.dma_start(qs[u][j][own, :].bitcast(F32), q_part[q, :].bitcast(F32)).then_inc(op_in, 16)
                            sp.dma_start(ks[u][j][own, :].bitcast(F32), k_part[kk, :].bitcast(F32)).then_inc(op_in, 16)

                def weights(k, u):
                    sp.wait_ge(v_ps, k + 1)
                    sp.dma_start(wpair[u % 2][:], w_qkv[(u + 2) % PAIRS]).then_inc(w_in[u % 2], 16)

                operands(0, 0)
                weights(0, 0)
                sp.sem_inc(out_done, 1)
                with sp.Fori(0, B) as b:
                    nxt = sp.snap((b + 1) % B)
                    for u in range(PAIRS):
                        k = sp.snap(b * PAIRS + u + 1)
                        operands(k, (u + 1) % 2)
                        if u == 0:
                            sp.wait_ge(out_done, b * CC * 16 + 1)
                            sp.dma_start(res[:], y[bass.ds(b, 1)].rearrange("o p c n -> (o p) c n")).then_inc(r_in, 16)
                        weights(k, (u + 1) % PAIRS)
                        if u == PAIRS - 2:
                            sp.dma_start(xin[:], y[bass.ds(nxt, 1)].rearrange("o p c n -> (o p) c n")).then_inc(x_in, 16)
                    for c in range(CC):
                        sp.wait_ge(res_ok, b * CC + c + 2)
                        sp.dma_start(out[bass.ds(b, 1), c * P:(c + 1) * P, :].rearrange("o p n -> (o p) n"),
                                     res[:, c, :]).then_inc(out_done, 16)
                sp.wait_ge(out_done, B * CC * 16 + 1)
                sp.wait_ge(x_in, (B + 1) * 16)
                for u in range(2):
                    sp.wait_ge(w_in[u], (B * PAIRS // 2 + 1 + (u == 0)) * 16)
                sp.wait_ge(op_in, (B * PAIRS + 1) * MOVES)

            @block.tensor
            def _(pe):
                def chunk_product(dst, w, src, done):
                    for g in range(NH):
                        for c in range(CC):
                            mm = pe.matmul(halves(dst, g), w(c), halves(src(c), g), start=c == 0, stop=c == CC - 1)
                    mm.then_inc(done, 1)

                def qk_quarter(k, u, n):
                    g = n // 2
                    for c in range(2 * (n % 2), 2 * (n % 2) + 2):
                        mm = pe.matmul(halves(ps_p, g), wpair[u % 2][:, c, 0:P], halves(xin[:, c, :], g),
                                       start=c == 0, stop=c == CC - 1)
                    if n == 3:
                        mm.then_inc(qk_ps, 1)

                def v_tiles(k, u, tiles):
                    for m in tiles:
                        for c in range(CC):
                            mm = pe.matmul(ps_p[:, m * P:(m + 1) * P], xin[:, c, m * P:(m + 1) * P],
                                           wpair[u % 2][:, c, P:2 * P], start=c == 0, stop=c == CC - 1)
                    if m == NT - 1:
                        mm.then_inc(v_ps, 1)

                def scores(it, u, t):
                    for j in range(2):
                        pe.wait_ge(exp_ok, it * TILES + 2 * t + j + 1)
                        for g in range(NH):
                            mm = pe.matmul(halves(ps_s[j], g), ks[u % 2][j][:, t * P:(t + 1) * P],
                                           halves(qs[u % 2][j], g), start=True, stop=True)
                        mm.then_inc(s_ps, 1)

                def weigh(it, t):
                    if t == 0:
                        pe.wait_ge(at_ok, it + 1)
                    pe.wait_ge(vs_ok, it * NT + t + 1)
                    for g in range(NH):
                        for j in range(2):
                            mm = pe.matmul(halves(ps_o[D * j:D * j + D], g), vs[:, t % 2, j, :],
                                           halves(prob[:, t % 2, j, :], g), start=t == 0, stop=t == NT - 1)
                    mm.then_inc(o_ps, 1)

                pe.wait_ge(const_in, 5 * 16)
                pe.wait_ge(x_in, 16)
                pe.wait_ge(w_in[0], 16)
                for n in range(4):
                    qk_quarter(0, 0, n)
                pe.wait_ge(full_ok, 1)
                v_tiles(0, 0, range(NT))
                with pe.Fori(0, B) as b:
                    for u in range(PAIRS):
                        it = pe.snap(b * PAIRS + u)
                        k, last = it + 1, u == PAIRS - 1
                        if u == 0:
                            pe.wait_ge(res_ok, b * CC + 1)
                            pe.wait_ge(op_in, (it + 1) * MOVES)
                            scores(it, u, 0)
                        for t in range(NT):
                            if t < NT - 1:
                                scores(it, u, t + 1)
                            elif not last:
                                pe.wait_ge(op_in, (it + 2) * MOVES)
                                scores(it + 1, u + 1, 0)
                            weigh(it, t)
                            n = t - (V_STEP if last else QK_STEP)
                            if 0 <= n < 4:
                                if n == 0:
                                    pe.wait_ge(v_ok, it + 1)
                                    pe.wait_ge(w_in[(u + 1) % 2], (b * 2 + (u + 1) // 2 + 1) * 16)
                                    if last:
                                        pe.wait_ge(x_in, (b + 2) * 16)
                                qk_quarter(k, u + 1, n)
                            elif not last and t < V_STEP + len(V_TILES):
                                if t == V_STEP:
                                    pe.wait_ge(full_ok, it + 2)
                                v_tiles(k, u + 1, V_TILES[t - V_STEP])
                    pe.wait_ge(at_ok, (b + 1) * PAIRS + 1)
                    for o in range(CC):
                        if o >= 2:
                            pe.wait_ge(z_ok, b * CC + o - 1)
                        chunk_product(ps_s[o % 2], lambda c: w1[:, c, o * P:(o + 1) * P],
                                      lambda c: attn[:, c, :], h_ps)
                    pe.wait_ge(full_ok, (b + 1) * PAIRS + 1)
                    v_tiles(0, 0, range(NT))
                    pe.wait_ge(z_ok, (b + 1) * CC)
                    for c in range(CC):
                        pe.wait_ge(mish_ok, b * CC + c + 1)
                        for o in range(2):
                            for g in range(NH):
                                mm = pe.matmul(halves(ps_s[o], g), w2[:, c, o * P:(o + 1) * P], halves(hid[:, c, :], g),
                                               start=c == 0, stop=c == CC - 1)
                            if c == CC - 1:
                                mm.then_inc(r_ps, 1)
                    for o in range(2, CC):
                        pe.wait_ge(res_ok, b * CC + o)
                        chunk_product(ps_s[o % 2], lambda c: w2[:, c, o * P:(o + 1) * P],
                                      lambda c: hid[:, c, :], r_ps)

            @block.scalar
            def _(act):
                act.sem_inc(exp_ok, 2)
                act.sem_inc(at_ok, 1)
                act.wait_ge(const_in, 5 * 16)

                def exps(it, t):
                    for j in range(2):
                        i = 2 * t + j
                        act.wait_ge(nms_ok, it * TILES + i + 1)
                        act.wait_ge(o_ps, it * NT + t + 1)
                        act.activation(prob[:, t % 2, j, :], ps_s[j][:], ACT.Exp, bias=nms[:, i:i + 1],
                                       scale=SCALE1, accum_out=zsum[:, i:i + 1]).then_inc(exp_ok, 1)

                with act.Fori(0, B) as b:
                    exps(act.snap(b * PAIRS), 0)
                    for u in range(PAIRS):
                        it = act.snap(b * PAIRS + u)
                        for t in range(1, NT):
                            exps(it, t)
                        if u < PAIRS - 1:
                            exps(it + 1, 0)
                        act.wait_ge(o_ps, (it + 1) * NT + 2)
                        act.activation(attn[:, u, :], ps_o[:], ACT.Identity).then_inc(at_ok, 1)
                    for c in range(CC):
                        act.wait_ge(h_ps, b * CC + c + 1)
                        if c:
                            act.wait_ge(mish_ok, b * CC + c)
                        act.activation(z[:], ps_s[c % 2][:], ACT.Identity,
                                       bias=vecs[:, V1["b1"] + c:V1["b1"] + c + 1]).then_inc(z_ok, 1)
                        act.wait_ge(zc_ok, b * CC + c + 1)
                        act.activation(e[:], e[:], ACT.Exp).then_inc(e_ok, 1)
                        act.wait_ge(num_ok, b * CC + c + 1)
                        act.activation(inv[:], num[:], ACT.Ln, bias=two[:]).then_inc(ln_ok, 1)
                        act.wait_ge(ln_ok, b * CC + c + 1)
                        act.activation(inv[:], inv[:], ACT.Exp, scale=-1.0).then_inc(inv_ok, 1)

            @block.vector
            def _(dve):
                dve.sem_inc(res_ok, 1)
                dve.memset(two[:], 2.0)
                dve.sem_inc(o_ps, 2)
                dve.wait_ge(const_in, 5 * 16)

                def qk_full(k, u):
                    dve.wait_ge(qk_ps, k + 1)
                    dve.scalar_tensor_tensor(full[:], ps_p[:], vecs[:, V1["bqk"] + u:V1["bqk"] + u + 1],
                                             pos[:], ALU.add, ALU.add).then_inc(full_ok, 1)

                def qk_high(k):
                    dve.wait_ge(full_ok, k + 1)
                    if k is not FIRST:
                        dve.wait_ge(op_in, k * MOVES)
                    dve.tensor_copy(high[:], full[:]).then_inc(high_ok, 1)

                def qk_low(k):
                    dve.wait_ge(high_ok, k + 1)
                    dve.tensor_tensor(low[:], full[:], high[:].bitcast(F32), ALU.subtract).then_inc(low_ok, 1)

                def pair_values(k, u):
                    dve.wait_ge(v_ps, k + 1)
                    dve.tensor_tensor(vt[u % 2][:], ps_p[:].rearrange("p (m n) -> p m n", m=NT),
                                      bv[:, u * P:(u + 1) * P].rearrange("p (o n) -> p o n", o=1)
                                      .broadcast_to([P, NT, P]), ALU.add).then_inc(v_ok, 1)

                def maxima(it, t):
                    for j in range(2):
                        i = 2 * t + j
                        dve.wait_ge(s_ps, it * TILES + i + 1)
                        dve.tensor_reduce(nmax[:, i:i + 1], ps_s[j][:], AX_X, ALU.max,
                                          negate=True).then_inc(max_ok, 1)
                        dve.wait_ge(max_ok, it * TILES + i + 1)
                        dve.tensor_scalar(nms[:, i:i + 1], nmax[:, i:i + 1], SCALE1, None,
                                          ALU.mult).then_inc(nms_ok, 1)

                def scaled(it, u, t):
                    dve.wait_ge(exp_ok, it * TILES + 2 * t + 4)
                    dve.reciprocal(zinv[:, 2 * t:2 * t + 2], zsum[:, 2 * t:2 * t + 2]).then_inc(zinv_ok, 1)
                    dve.wait_ge(zinv_ok, it * NT + t + 1)
                    dve.wait_ge(o_ps, it * NT + t + 1)
                    for j in range(2):
                        last = dve.tensor_scalar(vs[:, t % 2, j, :], vt[u % 2][:, t, D * j:D * j + D],
                                                 zinv[:, 2 * t + j:2 * t + j + 1], None, ALU.mult)
                    last.then_inc(vs_ok, 1)

                qk_full(0, 0)
                qk_high(FIRST)
                qk_low(0)
                pair_values(0, 0)
                with dve.Fori(0, B) as b:
                    maxima(dve.snap(b * PAIRS), 0)
                    for u in range(PAIRS):
                        it = dve.snap(b * PAIRS + u)
                        last = u == PAIRS - 1
                        for t in range(NT):
                            scaled(it, u, t)
                            if t == V_STEP and not last:
                                qk_full(it + 1, u + 1)
                            if t < NT - 1:
                                maxima(it, t + 1)
                            elif not last:
                                pair_values(it + 1, u + 1)
                                maxima(it + 1, 0)
                            if t == V_STEP and not last:
                                qk_high(it + 1)
                                qk_low(it + 1)
                    qk_full(it + 1, 0)
                    qk_high(it + 1)
                    qk_low(it + 1)
                    for c in range(CC):
                        def step(ins, n):
                            ins.then_inc(mchain, 1)
                            dve.wait_ge(mchain, (b * CC + c) * 3 + n)
                        dve.wait_ge(z_ok, b * CC + c + 1)
                        dve.tensor_scalar(e[:], z[:], MISH_TOP, None, ALU.min).then_inc(zc_ok, 1)
                        dve.wait_ge(e_ok, b * CC + c + 1)
                        dve.scalar_tensor_tensor(num[:], e[:], 2.0, e[:], ALU.add, ALU.mult).then_inc(num_ok, 1)
                        dve.wait_ge(inv_ok, b * CC + c + 1)
                        step(dve.scalar_tensor_tensor(e[:], num[:], 2.0, inv[:], ALU.add, ALU.mult), 1)
                        step(dve.scalar_tensor_tensor(e[:], e[:], 2.0, inv[:], ALU.subtract, ALU.mult), 2)
                        step(dve.tensor_tensor(num[:], num[:], e[:], ALU.mult), 3)
                        dve.scalar_tensor_tensor(hid[:, c, :], num[:], -1.0, z[:], ALU.mult, ALU.mult).then_inc(mish_ok, 1)
                    pair_values(it + 1, 0)
                    dve.wait_ge(r_in, (b + 1) * 16)
                    for c in range(CC):
                        dve.wait_ge(r_ps, b * CC + c + 1)
                        dve.scalar_tensor_tensor(res[:, c, :], ps_s[c % 2][:], vecs[:, V1["b2"] + c:V1["b2"] + c + 1],
                                                 res[:, c, :], ALU.add, ALU.add).then_inc(res_ok, 1)


def build(nc, x, w0_qkv, w0_out, vec0, w_sp, b_sp, w_se1, b_se1, w_se2, ident, w1_qkv, w1, w2, vec1, bv1, pos, out):
    mask_d = nc.dram_tensor("mask_rows", (HEADS, 4, N), F32, kind="Internal").ap()
    y = nc.dram_tensor("layer0_out", (B, P, CC, N), F32, kind="Internal").ap()
    layer0(nc, x, w0_qkv, w0_out, vec0, w_sp, b_sp, w_se1, b_se1, w_se2, ident, mask_d, y)
    layer1(nc, y, w1_qkv, w1, w2, vec1, bv1, pos, out)


def kernel(**inputs):
    import numpy as np
    import concourse.bacc as bacc
    from concourse.bass_utils import run_bass_kernel_spmd

    def arr(name):
        return np.asarray(inputs[name])

    def turned(w):
        return np.ascontiguousarray(w.T.reshape(CC, P, w.shape[0]).transpose(1, 0, 2))

    def columns(v):
        return v.reshape(-1, P).T

    l0 = {k: arr(f"L0_conv_{k}") for k in ("Wq", "Wk", "Wv", "Wo", "Wsp", "Wse1", "Wse2", "bq", "bk", "bv", "bo",
                                            "bsp", "bse1", "bse2", "gamma", "beta")}
    l1 = {k: arr(f"L1_conv_{k}") for k in ("PE", "Wq", "Wk", "Wv", "W1", "W2", "bq", "bk", "bv", "b1", "b2")}

    def by_pair(*ws):
        parts = [turned(w).reshape(P, CC, PAIRS, -1).transpose(2, 0, 1, 3) for w in ws]
        return np.ascontiguousarray(np.concatenate(parts, axis=3))

    bqk = np.concatenate([l1["bq"].reshape(PAIRS, QS1), l1["bk"].reshape(PAIRS, QS1)], axis=1).T
    given = {
        "x": np.ascontiguousarray(arr("x").reshape(B, CC, P, N).transpose(0, 2, 1, 3)),
        "w0_qkv": by_pair(l0["Wq"], l0["Wk"], l0["Wv"]),
        "w0_out": turned(l0["Wo"]),
        "vec0": np.ascontiguousarray(np.concatenate([columns(l0[k]) for k in V0], axis=1)),
        "w_sp": turned(l0["Wsp"]),
        "b_sp": np.ascontiguousarray(l0["bsp"].reshape(HEADS, 1)),
        "w_se1": turned(l0["Wse1"]),
        "b_se1": np.ascontiguousarray(l0["bse1"].reshape(SE, 1)),
        "w_se2": np.ascontiguousarray(l0["Wse2"].T),
        "ident": np.eye(P, dtype=np.float32),
        "w1_qkv": by_pair(l1["Wq"], l1["Wk"], l1["Wv"]),
        "w1": turned(l1["W1"]),
        "w2": turned(l1["W2"]),
        "vec1": np.ascontiguousarray(np.concatenate([bqk, columns(l1["b1"]), columns(l1["b2"])], axis=1)),
        "bv1": np.ascontiguousarray(l1["bv"]),
        "pos": np.ascontiguousarray(np.concatenate([l1["PE"].reshape(DQ, N)] * (P // DQ), axis=0)),
    }
    nc = bacc.Bacc("TRN2", target_bir_lowering=False, num_devices=1)
    args = [nc.dram_tensor(f"in_{k}", v.shape, F32, kind="ExternalInput").ap() for k, v in given.items()]
    out = nc.dram_tensor("out_0", (B, C, N), F32, kind="ExternalOutput").ap()
    build(nc, *args, out)
    r = run_bass_kernel_spmd(nc, [{f"in_{k}": v for k, v in given.items()}], core_ids=[0])
    return r.results[0]["out_0"].reshape(B, C, H, W)
```

```python
from contextlib import ExitStack

import concourse.bass as bass
from concourse import mybir

F32 = mybir.dt.float32
F32R = mybir.dt.float32r
ALU = mybir.AluOpType
ACT = mybir.ActivationFunctionType
AX_X = mybir.AxisListType.X

P = 128
B, C, H, W = 8, 512, 32, 32
N = H * W
HALF = 512
NH = N // HALF
CC = C // P
HEADS = 8
PAIRS = HEADS // 2
D = C // HEADS
NT = N // P
TILES = 2 * NT
GT = TILES // NH
SE = C // 16
G = 7
NEG = -1000000000.0
NEG_HI = float(round(NEG / 2 ** 18) * 2 ** 18)
NEG_LO = NEG - NEG_HI
DQ = 32
QS1 = 2 * DQ
SCALE0 = D ** -0.5
SCALE1 = 1.0 / float(DQ) ** 0.5
LN_EPS = 1e-5
FIRST = 0
MISH_TOP = 20.0

V0 = {name: i * CC for i, name in enumerate(["bq", "bk", "bv", "bo", "bse2", "gamma", "beta"])}
V1 = {name: i * CC for i, name in enumerate(["bqk", "b1", "b2"])}


def bins(n):
    return [(i * n // G, -(-(i + 1) * n // G)) for i in range(G)]


def spread(n):
    cell = [i * G // n for i in range(n)]
    return [(cell.index(g), n - cell[::-1].index(g)) for g in range(G)]


def layer0(nc, x, w_qkv, w_out, vec, w_sp, b_sp, w_se1, b_se1, w_se2, ident_d, mask_d, y):
    with ExitStack() as ctx:
        def sb(name, shape, dt=F32):
            return ctx.enter_context(nc.sbuf_tensor(name, shape, dt))

        def ps(name, shape):
            return ctx.enter_context(nc.psum_tensor(name, shape, F32))

        def sem(name):
            return ctx.enter_context(nc.semaphore(name))

        ident = sb("ident0", [P, P])
        mean_w = sb("mean_w", [P, P])
        ones = sb("ones", [P, D])
        wo = sb("wo", [P, CC, C])
        vecs = sb("vecs0", [P, len(V0) * CC])
        eps = sb("eps", [P, 1])
        bias = sb("bias", [P, 2])
        wsp = sb("wsp", [P, CC, HEADS])
        bsp = sb("bsp", [HEADS, 2])
        wse1 = sb("wse1", [P, CC, SE])
        bse1 = sb("bse1", [SE, 1])
        wse2 = sb("wse2", [SE, C])
        wqk = sb("wqk", [P, CC, 2 * P])
        wv = sb("wv", [P, CC, P])
        xraw = sb("xraw", [P, CC, N])
        xf = sb("xf", [P, CC, N])
        attn = sb("attn0", [P, CC, N])
        yt = sb("yt", [P, CC, N])
        total = sb("total", [P, N])
        std = sb("std", [P, NT])
        istd = sb("istd", [P, NT])
        gate = sb("gate", [HEADS, N])
        rows = sb("rows", [HEADS, G, W])
        cells = sb("cells", [HEADS, G, G])
        wide = sb("wide", [HEADS, G, W])
        mrow = sb("mrow", [HEADS, 3, N])
        pooled = sb("pooled", [P, CC])
        hid = sb("hid", [SE, 1])
        sez = sb("sez", [P, CC])
        cw = sb("cw", [P, CC])
        full = sb("full", [P, HALF])
        high = [sb(f"qk_high{o}", [P, N], F32R) for o in range(2)]
        low = [sb(f"qk_low{o}", [P, N], F32R) for o in range(2)]
        q1 = [sb(f"q1_{j}", [P, N], F32R) for j in range(2)]
        k1 = [sb(f"k1_{j}", [P, N], F32R) for j in range(2)]
        qk2 = sb("qk2", [D + 4, 2, 2, N], F32R)
        q2, k2 = ([qk2[:, o, j, :] for j in range(2)] for o in range(2))
        vt = sb("vt0", [P, NT, P])
        prob = sb("prob", [P, 2, N])
        pt = sb("pt", [P, 2, NT, HALF])
        nmax = sb("nmax0", [P, TILES])
        zsum = sb("zsum0", [P, TILES])
        zinv = sb("zinv0", [P, TILES])
        zdiag = sb("zdiag", [P, 2, HALF])
        zrow = sb("zrow", [P, HALF])

        ps_s = [ps(f"ps_s{i}", [P, N]) for i in range(2)]
        ps_t = ps("ps_t", [P, N])
        ps_o = ps("ps_o", [P, HALF])
        ps_p = ps("ps_p", [P, HALF])
        v_dst = (ps_s[1][:, 0:HALF], ps_p[:])
        wo_dst = (ps_s[0], ps_s[1], ps_t, ps_s[0])

        const_in = sem("const_in")
        wsp_in = sem("wsp_in")
        ident_in = sem("ident_in")
        wo_in = sem("wo_in")
        const_ok = sem("const_ok")
        x_in = sem("x_in")
        wqk_in, wv_in = sem("wqk_in"), sem("wv_in")
        mask_out = sem("mask_out")
        mask_in = sem("mask_in")
        q_in, k_in = sem("q_in"), sem("k_in")
        y_out = sem("y_out")
        sp_ps = sem("sp_ps")
        sp_e = sem("sp_e")
        mask_ok = sem("mask_ok")
        pool_ok = sem("pool_ok")
        se1_ps, hid_ok, se2_ps, sez_ok, see_ok = (sem(n) for n in ("se1_ps", "hid_ok", "se2_ps", "sez_ok", "see_ok"))
        cw_ok = sem("cw_ok")
        xf_ok = sem("xf_ok")
        qk_ps = sem("qk_ps")
        full_ok = sem("full_ok")
        high_ok = sem("high_ok")
        low_ok = sem("low_ok")
        bias_ok = sem("bias_ok")
        v_ps = sem("v_ps")
        v_ok = sem("v_ok")
        s_ps = sem("s_ps")
        max_ok = sem("max_ok")
        exp_ok = sem("exp_ok")
        t_ps = sem("t_ps")
        pt_a, pt_d = sem("pt_a"), sem("pt_d")
        zinv_ok = sem("zinv_ok")
        diag_ok = sem("diag_ok")
        o_ps = sem("o_ps")
        zrow_ok = sem("zrow_ok")
        mul_ok = sem("mul_ok")
        at_ok = sem("at_ok")
        part_ps = sem("part_ps")
        part_ok = sem("part_ok")
        wo_ps = sem("wo_ps")
        y_ok = sem("y_ok")
        mean_ps, var_ps = sem("mean_ps"), sem("var_ps")
        sum_ok = sem("sum_ok")
        rstd_ps = sem("rstd_ps")
        cen_ok, sq_ok, std_ok, istd_ok, rstd_ok, nrm_ok, gamma_ok, res_ok = (
            sem(n) for n in ("cen_ok", "sq_ok", "std_ok", "istd_ok", "rstd_ok", "nrm_ok", "gamma_ok", "res_ok"))
        SUMS = 2 * (CC - 1)
        dchain = sem("dchain0")
        COPIES = 6 * 16
        MASK_COPIES = 2 * 16

        def vec_at(name, c):
            return vecs[:, V0[name] + c:V0[name] + c + 1]

        def halves(t, g):
            return t[:, g * HALF:(g + 1) * HALF]

        QK_AT = {i: [] for i in range(TILES)}
        for n in range(4 * CC):
            QK_AT[1 + n // 2 if n < 4 else n - 1 if n != 8 else n].append((n // CC, n % CC))
        ENDS = {i: n for i in range(TILES) for n, c in QK_AT[i] if c == CC - 1}
        SP_AT = (1, 2)
        POOL_AT = range(CC)
        SQUEEZE_AT, EXCITE_AT, GATE_AT = 10, 11, 12
        PARTS = NH * CC
        PART_AT = (3, 4, 5, 8, 9, 10, 11, 12)
        PSUM_QK = (1, 1, 0, 0)

        with nc.Block() as block:

            @block.sync
            def _(sp):
                sp.dma_start(wsp[:], w_sp).then_inc(wsp_in, 16)
                for c in range(CC):
                    sp.dma_start(xraw[:, c, :], x[0, :, c, :]).then_inc(x_in, 16)
                for dst, src in ((bsp[:, 0:1], b_sp), (vecs[:], vec), (wse1[:], w_se1),
                                 (bse1[:], b_se1), (wse2[:], w_se2)):
                    sp.dma_start(dst, src).then_inc(const_in, 16)

                def load_qk(pair):
                    sp.dma_start(wqk[:], w_qkv[pair, :, :, 0:2 * P].rearrange("o p c n -> (o p) c n")).then_inc(wqk_in, 16)

                def load_v(pair):
                    sp.dma_start(wv[:], w_qkv[pair, :, :, 2 * P:].rearrange("o p c n -> (o p) c n")).then_inc(wv_in, 16)

                load_qk(slice(0, 1))
                load_v(slice(0, 1))
                sp.dma_start(ident[:], ident_d).then_inc(ident_in, 16)
                sp.dma_start(wo[:], w_out).then_inc(wo_in, 16)
                sp.wait_ge(const_ok, 1)

                def gates(k, nxt):
                    sp.wait_ge(mask_ok, k + 1)
                    sp.dma_start(mask_d[:, 1:4, :], mrow[:]).then_inc(mask_out, 16)
                    sp.dma_start(mask_d[:, 0:1, :], mrow[:, 0:1, :]).then_inc(mask_out, 16)
                    sp.wait_ge(xf_ok, (k + 1) * CC)
                    sp.dma_start(xraw[:], x[nxt].rearrange("o p c n -> (o p) c n")).then_inc(x_in, 16)
                    sp.wait_ge(mask_out, (k + 1) * 32)

                def query_operands(k, own_pair):
                    if k is not FIRST:
                        sp.wait_ge(v_ps, k * 2)
                        load_v(own_pair)
                        sp.wait_ge(s_ps, k * TILES)
                    sp.wait_ge(low_ok, k * 4 + 2)
                    for j in range(2):
                        own = slice(D * j, D * j + D)
                        sp.dma_start(q1[j][0:D, :].bitcast(F32), high[0][own, :].bitcast(F32)).then_inc(q_in, 16)
                        sp.dma_start(q1[j][D:P, :].bitcast(F32), low[0][own, :].bitcast(F32)).then_inc(q_in, 16)
                        sp.dma_start(q2[j][0:D, :].bitcast(F32), high[0][own, :].bitcast(F32)).then_inc(q_in, 16)

                def key_operands(k, p, nxt):
                    both = mask_d[bass.ds(p * 2, 2)].rearrange("j r n -> r j n")
                    sp.dma_start(qk2[D:D + 2, 0, :, :].bitcast(F32), both[2:4]).then_inc(mask_in, 16)
                    sp.dma_start(qk2[D:D + 4, 1, :, :].bitcast(F32), both).then_inc(mask_in, 16)
                    sp.wait_ge(low_ok, k * 4 + 4)
                    for j in range(2):
                        own = slice(D * j, D * j + D)
                        sp.dma_start(k1[j][0:D, :].bitcast(F32), high[1][own, :].bitcast(F32)).then_inc(k_in, 16)
                        sp.dma_start(k1[j][D:P, :].bitcast(F32), high[1][own, :].bitcast(F32)).then_inc(k_in, 16)
                        sp.dma_start(k2[j][0:D, :].bitcast(F32), low[1][own, :].bitcast(F32)).then_inc(k_in, 16)
                    load_qk(nxt)

                query_operands(FIRST, None)
                gates(0, slice(1, 2))
                key_operands(FIRST, 0, slice(1, 2))
                with sp.Fori(0, B) as b:
                    ahead = sp.snap((b + 2) % B)
                    with sp.Fori(0, PAIRS - 1) as p:
                        nxt = sp.snap((p + 2) % PAIRS)
                        k = sp.snap(b * PAIRS + p + 1)
                        query_operands(k, bass.ds(p + 1, 1))
                        key_operands(k, p + 1, bass.ds(nxt, 1))
                    gates(sp.snap(b + 1), bass.ds(ahead, 1))
                    k = sp.snap(b * PAIRS + PAIRS)
                    query_operands(k, slice(0, 1))
                    key_operands(k, 0, slice(1, 2))
                    for c in range(CC):
                        sp.wait_ge(res_ok, b * CC + c + 1)
                        sp.dma_start(y[bass.ds(b, 1), :, c, :].rearrange("o p n -> (o p) n"),
                                     yt[:, c, :]).then_inc(y_out, 16)
                sp.wait_ge(y_out, B * CC * 16 + 1)
                sp.wait_ge(x_in, (B + 1 + CC) * 16)
                sp.wait_ge(wqk_in, (B * PAIRS + 2) * 16)
                sp.wait_ge(wv_in, (B * PAIRS + 1) * 16)
                sp.wait_ge(mask_in, (B * PAIRS + 1) * MASK_COPIES)
                sp.wait_ge(q_in, (B * PAIRS + 1) * COPIES)
                sp.wait_ge(k_in, (B * PAIRS + 1) * COPIES)

            @block.tensor
            def _(pe):
                def spatial(k, g):
                    if g:
                        pe.wait_ge(sp_e, k * 2 + 1)
                    elif k is not FIRST:
                        pe.wait_ge(v_ok, (k * PAIRS) * 2)
                    pe.wait_ge(x_in, (k + CC) * 16)
                    for c in range(CC):
                        mm = pe.matmul(ps_p[0:HEADS, :], wsp[:, c, :], halves(xraw[:, c, :], g),
                                       start=c == 0, stop=c == CC - 1)
                    mm.then_inc(sp_ps, 1)

                def squeeze(k):
                    pe.wait_ge(pool_ok, (k + 1) * CC)
                    for c in range(CC):
                        mm = pe.matmul(ps_o[0:SE, 0:1], wse1[:, c, :], pooled[:, c:c + 1],
                                       start=c == 0, stop=c == CC - 1)
                    mm.then_inc(se1_ps, 1)

                def excite(k):
                    pe.wait_ge(hid_ok, k + 1)
                    for c in range(CC):
                        mm = pe.matmul(ps_o[:, 1 + c:2 + c], wse2[:, c * P:(c + 1) * P], hid[:],
                                       start=True, stop=True)
                    mm.then_inc(se2_ps, 1)

                def quarter(k, n, c, dst):
                    if n == 0 and c == 0:
                        pe.wait_ge(wqk_in, (k + 1) * 16)
                    mm = pe.matmul(dst, wqk[:, c, n // NH * P:(n // NH + 1) * P], halves(xf[:, c, :], n % NH),
                                   start=c == 0, stop=c == CC - 1)
                    if c == CC - 1:
                        mm.then_inc(qk_ps, 1)

                def queries_keys(k, n):
                    for c in range(CC):
                        quarter(k, n, c, halves(ps_s[PSUM_QK[n]], n % NH))

                def attend(it, last):
                    def values(g):
                        if g:
                            pe.wait_ge(zrow_ok, it * NH + 1)
                        else:
                            pe.wait_ge(wv_in, (it + 1) * 16)
                            pe.wait_ge(full_ok, (it + 1) * 4)
                        for m in range(4):
                            for c in range(CC):
                                mm = pe.matmul(v_dst[g][:, m * P:(m + 1) * P],
                                               xf[:, c, (4 * g + m) * P:(4 * g + m + 1) * P],
                                               wv[:, c, :], start=c == 0, stop=c == CC - 1)
                        mm.then_inc(v_ps, 1)

                    def scores(i):
                        j, t = i % 2, i // 2
                        if i >= 2:
                            pe.wait_ge(exp_ok, it * TILES + i - 1)
                        for g in range(NH):
                            pe.matmul(halves(ps_s[j], g), q1[j][:, t * P:(t + 1) * P], halves(k1[j], g),
                                      start=True, stop=False)
                            mm = pe.matmul(halves(ps_s[j], g), q2[j][:, t * P:(t + 1) * P], halves(k2[j], g),
                                           start=False, stop=True)
                        mm.then_inc(s_ps, 1)

                    def turn(i):
                        pe.wait_ge(exp_ok, it * TILES + i + 1)
                        for h, copied in ((0, pt_a), (1, pt_d)):
                            if i:
                                pe.wait_ge(copied, it * TILES + i)
                            for m in range(4 * h, 4 * h + 4):
                                mm = pe.transpose(ps_t[:, m * P:(m + 1) * P], prob[:, i % 2, m * P:(m + 1) * P],
                                                  ident[:])
                            mm.then_inc(t_ps, 1)

                    def weigh(g):
                        end = GT * g + GT - 1
                        pe.wait_ge(pt_a, it * TILES + end + 1)
                        pe.wait_ge(pt_d, it * TILES + end + 1)
                        if g:
                            pe.wait_ge(at_ok, it * NH + g)
                            if last:
                                pe.wait_ge(sez_ok, b + 2)
                        else:
                            pe.wait_ge(v_ok, it * 2 + 2)
                        for m in range(NT):
                            for j in range(2):
                                own = slice(D * j, D * j + D)
                                pe.matmul(ps_o[own, :], vt[:, m, own], pt[:, j, m, :],
                                          start=m == 0, stop=m == NT - 1)
                        pe.wait_ge(diag_ok, it * TILES + end + 1)
                        if last:
                            pe.wait_ge(part_ok, b * PARTS + (PARTS if g else 3))
                        else:
                            pe.wait_ge(full_ok, (it + 1) * 4 + 2 * g + 2)
                        for j in range(2):
                            mm = pe.matmul(ps_p[D * j:D * j + D, :], ones[:], zdiag[:, j, :], start=True, stop=True)
                        mm.then_inc(o_ps, 1)

                    def part(n):
                        if n == 0:
                            pe.wait_ge(wo_in, 16)
                            pe.wait_ge(at_ok, it * NH)
                            pe.wait_ge(sp_e, b * 2 + 4)
                        elif PART_AT[n - 1] < GT <= PART_AT[n]:
                            pe.wait_ge(zrow_ok, it * NH + 2)
                        else:
                            pe.wait_ge(part_ok, b * PARTS + n)
                        for c in range(CC - 1):
                            mm = pe.matmul(ps_p[:], wo[:, c, n // NH * P:(n // NH + 1) * P],
                                           halves(attn[:, c, :], n % NH), start=c == 0, stop=c == CC - 2)
                        mm.then_inc(part_ps, 1)

                    def filler(i):
                        if last:
                            if i in SP_AT:
                                spatial(b + 1, SP_AT.index(i))
                            if i in PART_AT:
                                part(PART_AT.index(i))
                            if i == SQUEEZE_AT:
                                pe.wait_ge(at_ok, it * NH + 1)
                                squeeze(b + 1)
                            if i == EXCITE_AT:
                                excite(b + 1)
                        else:
                            for n, c in QK_AT[i]:
                                if c == 0 and n == 0:
                                    pe.wait_ge(v_ok, it * 2 + 2)
                                elif c == 0 and n == 2:
                                    pe.wait_ge(zrow_ok, it * NH + 2)
                                elif c == 0:
                                    pe.wait_ge(full_ok, (it + 1) * 4 + n)
                                quarter(it + 1, n, c, ps_p[:])

                    values(0)
                    pe.wait_ge(q_in, (it + 1) * COPIES)
                    pe.wait_ge(mask_in, (it + 1) * MASK_COPIES)
                    pe.wait_ge(k_in, (it + 1) * COPIES)
                    scores(0)
                    pe.wait_ge(v_ok, it * 2 + 1)
                    scores(1)
                    values(1)
                    for i in range(TILES):
                        if i < TILES - 2 and i != GT:
                            scores(i + 2)
                        turn(i)
                        filler(i)
                        if i == GT - 1:
                            scores(i + 3)
                            weigh(0)
                    weigh(1)

                pe.wait_ge(wsp_in, 16)
                pe.sem_inc(o_ps, 1)
                for g in range(NH):
                    spatial(FIRST, g)
                pe.wait_ge(const_in, 5 * 16)
                pe.wait_ge(const_ok, 1)
                squeeze(0)
                excite(0)
                pe.wait_ge(xf_ok, CC)
                for n in range(4):
                    queries_keys(0, n)
                pe.wait_ge(ident_in, 16)
                with pe.Fori(0, B) as b:
                    with pe.Fori(0, PAIRS - 1) as p:
                        attend(pe.snap(b * PAIRS + p), False)
                    it = pe.snap(b * PAIRS + PAIRS - 1)
                    attend(it, True)
                    for g in range(NH):
                        if g:
                            pe.wait_ge(at_ok, (b + 1) * NH * PAIRS)
                        for o in range(CC - 1):
                            mm = pe.matmul(halves(wo_dst[o], g), wo[:, CC - 1, o * P:(o + 1) * P],
                                           halves(attn[:, CC - 1, :], g), start=True, stop=True)
                            if g:
                                mm.then_inc(wo_ps, 1)
                    pe.wait_ge(y_ok, b * CC + 1)
                    for g in range(NH):
                        mm = pe.matmul(halves(wo_dst[CC - 1], g), wo[:, CC - 1, (CC - 1) * P:],
                                       halves(attn[:, CC - 1, :], g), start=True, stop=True)
                    mm.then_inc(wo_ps, 1)
                    pe.wait_ge(xf_ok, (b + 2) * CC)
                    pe.wait_ge(y_ok, b * CC + 2)
                    for n in range(2):
                        queries_keys(it + 1, n)
                    pe.wait_ge(sum_ok, b * SUMS + CC - 1)
                    for g in range(NH):
                        mm = pe.matmul(halves(ps_t, g), mean_w[:], halves(total, g), start=True, stop=True)
                    mm.then_inc(mean_ps, 1)
                    for n in range(2, 4):
                        queries_keys(it + 1, n)
                    pe.wait_ge(sum_ok, (b + 1) * SUMS)
                    for t in range(NT):
                        mm = pe.matmul(ps_t[:, t:t + 1], total[:, t * P:(t + 1) * P], mean_w[:, 0:1],
                                       start=True, stop=True)
                    mm.then_inc(var_ps, 1)
                    pe.wait_ge(istd_ok, b + 1)
                    for t in range(NT):
                        mm = pe.matmul(ps_t[:, t * P:(t + 1) * P], istd[:, t:t + 1].broadcast_to([P, P]), ident[:],
                                       start=True, stop=True)
                    mm.then_inc(rstd_ps, 1)

            @block.scalar
            def _(act):
                def spatial(k, g):
                    act.wait_ge(sp_ps, k * 2 + g + 1)
                    act.activation(halves(gate, g), ps_p[0:HEADS, :], ACT.Exp, bias=bsp[:, 1:2],
                                   scale=-1.0).then_inc(sp_e, 1)

                def squeeze(k):
                    act.wait_ge(se1_ps, k + 1)
                    act.activation(hid[:], ps_o[0:SE, 0:1], ACT.Relu, bias=bse1[:],
                                   scale=1.0 / N).then_inc(hid_ok, 1)

                def excite(k):
                    act.wait_ge(sez_ok, k + 1)
                    act.activation(sez[:], sez[:], ACT.Exp, scale=-1.0).then_inc(see_ok, 1)

                def gated(k, c):
                    if c == 0:
                        act.wait_ge(cw_ok, k + 1)
                    if k is not FIRST:
                        act.wait_ge(part_ok, (k - 1) * PARTS + NH * (c + 1))
                    act.activation(xf[:, c, :], xraw[:, c, :], ACT.Identity, scale=cw[:, c:c + 1]).then_inc(xf_ok, 1)

                def biases(p):
                    act.activation(bias[:, 0:1], vecs[:, bass.ds(p + V0["bq"], 1)], ACT.Identity, scale=SCALE0)
                    act.activation(bias[:, 1:2], vecs[:, bass.ds(p + V0["bk"], 1)], ACT.Identity).then_inc(bias_ok, 1)

                def quarter(k, n, src):
                    if n == 0:
                        act.wait_ge(bias_ok, k + 1)
                    act.wait_ge(qk_ps, k * 4 + n + 1)
                    if n or k is not FIRST:
                        act.wait_ge(low_ok, k * 4 + n)
                    if n < NH:
                        ins = act.activation(full[:], src, ACT.Identity, bias=bias[:, 0:1], scale=SCALE0)
                    else:
                        ins = act.activation(full[:], src, ACT.Identity, bias=bias[:, 1:2])
                    ins.then_inc(full_ok, 1)

                def queries_keys(k, n):
                    quarter(k, n, halves(ps_s[PSUM_QK[n]], n % NH))

                def attend(it, p, last):
                    def values(g):
                        act.wait_ge(v_ps, it * 2 + g + 1)
                        act.activation(vt[:, 4 * g:4 * g + 4, :], v_dst[g].rearrange("p (m n) -> p m n", m=4),
                                       ACT.Identity).then_inc(v_ok, 1)

                    def exps(i):
                        act.wait_ge(max_ok, it * TILES + i + 1)
                        if i >= 2:
                            act.wait_ge(t_ps, (it * TILES + i) * 2 - 2)
                        act.activation(prob[:, i % 2, :], ps_s[i % 2][:], ACT.Exp, bias=nmax[:, i:i + 1],
                                       accum_out=zsum[:, i:i + 1]).then_inc(exp_ok, 1)

                    def copy_t(i):
                        act.wait_ge(t_ps, (it * TILES + i) * 2 + 1)
                        q = i // 2 % 4
                        act.activation(pt[:, i % 2, 0:4, q * P:(q + 1) * P],
                                       ps_t[:, 0:HALF].rearrange("p (m n) -> p m n", m=4),
                                       ACT.Identity).then_inc(pt_a, 1)

                    def copy_z(g):
                        act.wait_ge(o_ps, it * NH + g + 2)
                        if g:
                            act.wait_ge(mul_ok, it * NH + g)
                        act.activation(zrow[:], ps_p[:], ACT.Identity).then_inc(zrow_ok, 1)

                    values(0)
                    exps(0)
                    biases(0 if last else p + 1)
                    for i in range(TILES):
                        if i < TILES - 1:
                            exps(i + 1)
                        if i == 0:
                            values(1)
                        if i == GT:
                            copy_z(0)
                        copy_t(i)
                        if not last and i in ENDS:
                            quarter(it + 1, ENDS[i], ps_p[:])
                        elif last and i in SP_AT:
                            spatial(b + 1, SP_AT.index(i))
                        elif last and i == SQUEEZE_AT:
                            squeeze(b + 1)
                        elif last and i == GATE_AT:
                            excite(b + 1)
                        elif last and i > GATE_AT:
                            gated(b + 1, i - GATE_AT - 1)
                    copy_z(1)

                act.wait_ge(const_in, 5 * 16)
                act.wait_ge(const_ok, 1)
                for g in range(NH):
                    spatial(0, g)
                squeeze(0)
                excite(0)
                act.sem_inc(y_out, 1)
                act.sem_inc(zrow_ok, 1)
                for c in range(CC):
                    gated(FIRST, c)
                biases(0)
                for n in range(4):
                    queries_keys(FIRST, n)
                with act.Fori(0, B) as b:
                    with act.Fori(0, PAIRS - 1) as p:
                        attend(act.snap(b * PAIRS + p), p, False)
                    it = act.snap(b * PAIRS + PAIRS - 1)
                    attend(it, None, True)
                    gated(b + 1, CC - 1)
                    for n in range(2):
                        queries_keys(it + 1, n)
                    for c in range(CC):
                        act.wait_ge(cen_ok, b * CC + c + 1)
                        act.activation(attn[:, c, :], yt[:, c, :], ACT.Square).then_inc(sq_ok, 1)
                        if c >= CC - 2:
                            queries_keys(it + 1, c)
                    act.wait_ge(var_ps, b + 1)
                    act.activation(std[:], ps_t[:, 0:NT], ACT.Sqrt, bias=eps[:]).then_inc(std_ok, 1)
                    act.wait_ge(rstd_ps, b + 1)
                    act.activation(total[:], ps_t[:], ACT.Identity).then_inc(rstd_ok, 1)

            @block.vector
            def _(dve):
                ch = [0]
                MASK_STEPS = 9
                MASK_AT = {2: (0,), GT - 1: (1, 2, 3), 9: (4,), 10: (5,), TILES - 1: (6, 7, 8)}
                STEPS = 1 + 4 * 2 + 2 + 3 + 2

                def link(ins, k):
                    ch[0] += 1
                    ins.then_inc(dchain, 1)
                    dve.wait_ge(dchain, k * STEPS + ch[0])

                def pool(k, c):
                    dve.wait_ge(x_in, (k + CC) * 16)
                    dve.tensor_reduce(pooled[:, c:c + 1], xraw[:, c, :], AX_X, ALU.add).then_inc(pool_ok, 1)

                def excite(k):
                    dve.wait_ge(se2_ps, k + 1)
                    dve.tensor_tensor(sez[:], ps_o[:, 1:1 + CC], vecs[:, V0["bse2"]:V0["bse2"] + CC],
                                      ALU.add).then_inc(sez_ok, 1)
                    dve.wait_ge(see_ok, k + 1)
                    link(dve.tensor_scalar(sez[:], sez[:], 1.0, None, ALU.add), k)
                    dve.reciprocal(cw[:], sez[:]).then_inc(cw_ok, 1)

                def mask(k, steps):
                    for n in steps:
                        part = slice(n % 4 * N // 4, (n % 4 + 1) * N // 4)
                        if n < 4:
                            dve.wait_ge(sp_e, k * 2 + n // 2 + 1)
                            link(dve.tensor_scalar(gate[:, part], gate[:, part], 1.0, None, ALU.add), k)
                            last = dve.reciprocal(gate[:, part], gate[:, part])
                        elif n == 4:
                            pixels = gate[:].rearrange("p (h w) -> p w h", h=H)
                            for i, (lo, hi) in enumerate(bins(H)):
                                last = dve.tensor_reduce(rows[:, i, :], pixels[:, :, lo:hi], AX_X, ALU.add)
                            link(last, k)
                            for first in (0, 1):
                                size = bins(H)[first][1] - bins(H)[first][0]
                                last = dve.tensor_scalar(rows[:, first::2, :], rows[:, first::2, :], 1.0 / size, None,
                                                         ALU.mult)
                        elif n == 5:
                            for i, (lo, hi) in enumerate(bins(W)):
                                last = dve.tensor_reduce(cells[:, :, i:i + 1], rows[:, :, lo:hi], AX_X, ALU.add)
                            link(last, k)
                            for first in (0, 1):
                                size = bins(W)[first][1] - bins(W)[first][0]
                                last = dve.tensor_scalar(cells[:, :, first::2], cells[:, :, first::2], 1.0 / size, 0.5,
                                                         ALU.mult, ALU.is_gt)
                            link(last, k)
                            for lo, hi, i in ((*s, i) for i, s in enumerate(spread(W))):
                                last = dve.tensor_copy(wide[:, :, lo:hi],
                                                       cells[:, :, i:i + 1].broadcast_to([HEADS, G, hi - lo]))
                        else:
                            r = n - 6
                            scale, bias = ((1.0, 0.0), (-NEG_HI, NEG_HI), (-NEG_LO, NEG_LO))[r]
                            grid = mrow[:, r, :].rearrange("p (h w) -> p h w", h=H)
                            for i, (lo, hi) in enumerate(spread(H)):
                                last = dve.tensor_scalar(grid[:, lo:hi, :],
                                                         wide[:, i:i + 1, :].broadcast_to([HEADS, hi - lo, W]),
                                                         scale, bias, ALU.mult, ALU.add)
                        if n < MASK_STEPS - 1:
                            link(last, k)
                        else:
                            last.then_inc(mask_ok, 1)

                def split(k, n):
                    own = (n // NH, n % NH)
                    dve.wait_ge(full_ok, k * 4 + n + 1)
                    dve.tensor_copy(halves(high[own[0]], own[1]), full[:]).then_inc(high_ok, 1)
                    dve.wait_ge(high_ok, k * 4 + n + 1)
                    dve.tensor_tensor(halves(low[own[0]], own[1]), full[:], halves(high[own[0]], own[1]).bitcast(F32),
                                      ALU.subtract).then_inc(low_ok, 1)

                def part(b, n):
                    o, g = n // NH, n % NH
                    dve.wait_ge(part_ps, b * PARTS + n + 1)
                    if n == 0:
                        dve.wait_ge(y_out, b * CC * 16 + 1)
                    dve.scalar_tensor_tensor(halves(yt[:, o, :], g), ps_p[:], vec_at("bo", o), halves(xf[:, o, :], g),
                                             ALU.add, ALU.add).then_inc(part_ok, 1)

                def add_up(before, chunks, c):
                    if c > 1:
                        dve.wait_ge(sum_ok, before + c - 1)
                    dve.tensor_tensor(total[:], chunks[:, 0, :] if c == 1 else total[:], chunks[:, c, :],
                                      ALU.add).then_inc(sum_ok, 1)

                def attend(it, p, last):
                    def maxima(i):
                        dve.wait_ge(s_ps, it * TILES + i + 1)
                        dve.tensor_reduce(nmax[:, i:i + 1], ps_s[i % 2][:], AX_X, ALU.max,
                                          negate=True).then_inc(max_ok, 1)

                    def copy_t(i):
                        q = i // 2 % 4
                        dve.wait_ge(t_ps, (it * TILES + i) * 2 + 2)
                        dve.tensor_copy(pt[:, i % 2, 4:8, q * P:(q + 1) * P],
                                        ps_t[:, HALF:N].rearrange("p (m n) -> p m n", m=4)).then_inc(pt_d, 1)
                        dve.reciprocal(zinv[:, i:i + 1], zsum[:, i:i + 1]).then_inc(zinv_ok, 1)

                    def place(g):
                        dve.wait_ge(zrow_ok, it * NH + g + 2)
                        dst = attn[:, bass.ds(p, 1), g * HALF:(g + 1) * HALF].rearrange("p o n -> p (o n)")
                        dve.tensor_tensor(dst, ps_o[:], zrow[:], ALU.mult).then_inc(mul_ok, 1)
                        dve.wait_ge(mul_ok, it * NH + g + 1)
                        dve.tensor_scalar(dst, dst, vecs[:, bass.ds(p + V0["bv"], 1)], None,
                                          ALU.add).then_inc(at_ok, 1)

                    maxima(0)
                    maxima(1)
                    for i in range(TILES):
                        if i < TILES - 2:
                            maxima(i + 2)
                        copy_t(i)
                        if i == GT:
                            place(0)
                        if last and i in POOL_AT:
                            pool(b + 1, i)
                        if last and i == GATE_AT:
                            excite(b + 1)
                        if not last and i - 1 in ENDS:
                            split(it + 1, ENDS[i - 1])
                        if last and i in PART_AT:
                            part(b, PART_AT.index(i))
                        if last and i in MASK_AT:
                            mask(b + 1, MASK_AT[i])
                    place(1)

                dve.memset(mean_w[:], 1.0 / C)
                dve.memset(ones[:], 1.0)
                dve.memset(eps[:], LN_EPS)
                for j in range(2):
                    dve.memset(q2[j][D:D + 4, :].bitcast(F32), 1.0)
                dve.wait_ge(const_in, 5 * 16)
                dve.tensor_scalar(bsp[:, 1:2], bsp[:, 0:1], -1.0, None, ALU.mult).then_inc(const_ok, 1)
                for c in range(CC):
                    pool(FIRST, c)
                excite(0)
                for steps, n in ((range(4), 0), ((4, 5), 1), ((6, 7, 8), 2), ((), 3)):
                    mask(0, steps)
                    split(0, n)
                with dve.Fori(0, B) as b:
                    with dve.Fori(0, PAIRS - 1) as p:
                        attend(dve.snap(b * PAIRS + p), p, False)
                    it = dve.snap(b * PAIRS + PAIRS - 1)
                    ch[0] = 0
                    attend(it, PAIRS - 1, True)
                    assert ch[0] == STEPS, ch[0]
                    for c in range(CC):
                        dve.wait_ge(wo_ps, b * CC + c + 1)
                        dve.wait_ge(part_ok, b * PARTS + NH * (c + 1))
                        dve.tensor_tensor(yt[:, c, :], wo_dst[c][:], yt[:, c, :], ALU.add).then_inc(y_ok, 1)
                        if c:
                            dve.wait_ge(y_ok, b * CC + c + 1)
                            add_up(b * SUMS, yt, c)
                    for n in range(2):
                        split(it + 1, n)
                    dve.wait_ge(mean_ps, b + 1)
                    for c in range(CC):
                        dve.tensor_tensor(yt[:, c, :], yt[:, c, :], ps_t[:], ALU.subtract).then_inc(cen_ok, 1)
                    split(it + 1, 2)
                    dve.wait_ge(sq_ok, b * CC + 2)
                    add_up(b * SUMS + CC - 1, attn, 1)
                    split(it + 1, 3)
                    for c in range(2, CC):
                        dve.wait_ge(sq_ok, b * CC + c + 1)
                        add_up(b * SUMS + CC - 1, attn, c)
                    dve.wait_ge(std_ok, b + 1)
                    dve.reciprocal(istd[:], std[:]).then_inc(istd_ok, 1)

            @block.gpsimd
            def _(pool):
                pool.wait_ge(ident_in, 16)
                pool.wait_ge(const_in, 5 * 16)
                with pool.Fori(0, B) as b:
                    with pool.Fori(0, PAIRS) as p:
                        it = pool.snap(b * PAIRS + p)
                        for i in range(TILES):
                            if i % GT == 0:
                                pool.wait_ge(o_ps, it * NH + i // GT + 1)
                            pool.wait_ge(zinv_ok, it * TILES + i + 1)
                            q = i // 2 % 4
                            pool.tensor_tensor(zdiag[:, i % 2, q * P:(q + 1) * P], ident[:],
                                               zinv[:, i:i + 1].broadcast_to([P, P]), ALU.mult).then_inc(diag_ok, 1)
                    for c in range(CC):
                        pool.wait_ge(sq_ok, b * CC + c + 1)
                        pool.tensor_tensor(yt[:, c, :], yt[:, c, :], vec_at("gamma", c).broadcast_to([P, N]),
                                           ALU.mult).then_inc(gamma_ok, 1)
                    pool.wait_ge(rstd_ok, b + 1)
                    for c in range(CC):
                        pool.wait_ge(gamma_ok, b * CC + c + 1)
                        pool.tensor_tensor(yt[:, c, :], yt[:, c, :], total[:], ALU.mult).then_inc(nrm_ok, 1)
                        pool.wait_ge(nrm_ok, b * CC + c + 1)
                        pool.tensor_tensor(yt[:, c, :], yt[:, c, :], vec_at("beta", c).broadcast_to([P, N]),
                                           ALU.add).then_inc(res_ok, 1)


def layer1(nc, y, w_qkv, w1_d, w2_d, vec, bv_d, pe_d, out):
    with ExitStack() as ctx:
        def sb(name, shape, dt=F32):
            return ctx.enter_context(nc.sbuf_tensor(name, shape, dt))

        def ps(name, shape):
            return ctx.enter_context(nc.psum_tensor(name, shape, F32))

        def sem(name):
            return ctx.enter_context(nc.semaphore(name))

        w1 = sb("w1", [P, CC, C])
        w2 = sb("w2", [P, CC, C])
        vecs = sb("vecs1", [P, len(V1) * CC])
        bv = sb("bv1", [P, C])
        pos = sb("pos", [P, N])
        wpair = [sb(f"wpair1_{u}", [P, CC, 2 * P]) for u in range(2)]
        xin = sb("xin", [P, CC, N])
        full = sb("full1", [P, N])
        high = sb("high1", [P, N], F32R)
        low = sb("low1", [P, N], F32R)
        ks = [[sb(f"ks{u}_{j}", [P, N], F32R) for j in range(2)] for u in range(2)]
        qs = [[sb(f"qs{u}_{j}", [P, N], F32R) for j in range(2)] for u in range(2)]
        vt = [sb(f"vt1_{u}", [P, NT, P]) for u in range(2)]
        vs = sb("vs", [P, 2, 2, D])
        prob = sb("prob1", [P, 2, 2, N])
        attn = sb("attn1", [P, CC, N])
        hid = sb("hid1", [P, CC, N])
        e, num, inv = ([sb(f"{name}{i}", [P, N]) for i in range(2)] for name in ("e", "num", "inv"))
        two = sb("two", [P, 1])
        res = sb("res", [P, CC, N])
        nmax = sb("nmax1", [P, TILES])
        nms = sb("nms", [P, TILES])
        zsum = sb("zsum1", [P, TILES])
        zinv = sb("zinv1", [P, TILES])

        ps_s = [ps(f"ps1_s{i}", [P, N]) for i in range(2)]
        ps_o = ps("ps1_o", [P, N])
        ps_p = ps("ps1_p", [P, N])
        r_dst = (ps_s[0], ps_s[1], ps_o, ps_s[1])

        const_in = sem("const1_in")
        mlp_in = sem("mlp_in")
        x_in = sem("x1_in")
        r_in = sem("r1_in")
        w_in = [sem("w1_in0"), sem("w1_in1")]
        op_in = sem("op_in")
        out_done = sem("out_done")
        qk_ps = sem("qk1_ps")
        v_ps = sem("v1_ps")
        full_ok, high_ok, low_ok = sem("full1_ok"), sem("high1_ok"), sem("low1_ok")
        v_ok = sem("v1_ok")
        s_ps = sem("s1_ps")
        max_ok = sem("max1_ok")
        nms_ok = sem("nms_ok")
        exp_ok = sem("exp1_ok")
        zinv_ok = sem("zinv1_ok")
        vs_ok = sem("vs_ok")
        o_ps = sem("o1_ps")
        at_ok = sem("at1_ok")
        part_ps = sem("part1_ps")
        part_ok = sem("part1_ok")
        h_ps = sem("h_ps")
        z01_ok, z23_ok, zc_ok, e_ok, num_ok, ln_ok, inv_ok = (
            sem(n) for n in ("z01_ok", "z23_ok", "zc_ok", "e_ok", "num_ok", "ln_ok", "inv1_ok"))
        mish_ok = sem("mish_ok")
        r_ps = sem("r_ps")
        res_ok = sem("res1_ok")
        zn_ok = sem("zn_ok")
        newton_ok = sem("newton_ok")
        MOVES = 16 * 16
        QK_STEP, V_STEP = 0, 4
        V_TILES = ([0, 1, 2], [3, 4, 5], [6, 7])
        PARTS = 2 * NH
        V_BEFORE = {2: range(5)}
        V_MLP = 5

        def halves(t, g):
            return t[:, g * HALF:(g + 1) * HALF]

        with nc.Block() as block:

            @block.sync
            def _(sp):
                sp.dma_start(wpair[0][:], w_qkv[0]).then_inc(w_in[0], 16)
                sp.dma_start(xin[:], y[0]).then_inc(x_in, 16)
                for dst, src in ((vecs, vec), (pos, pe_d)):
                    sp.dma_start(dst[:], src).then_inc(const_in, 16)
                sp.dma_start(bv[:], bv_d.partition_broadcast(P)).then_inc(const_in, 16)
                sp.dma_start(wpair[1][:], w_qkv[1]).then_inc(w_in[1], 16)
                for dst, src in ((w1, w1_d), (w2, w2_d)):
                    sp.dma_start(dst[:], src).then_inc(mlp_in, 16)

                def operands(k, u):
                    for q_at, k_at, part, ready in (((0, 1), (0, 2), high, high_ok), ((2, 3), (1, 3), low, low_ok)):
                        sp.wait_ge(ready, k + 1)
                        for j in range(2):
                            for at in q_at:
                                sp.dma_start(qs[u][j][at * DQ:(at + 1) * DQ, :].bitcast(F32),
                                             part[DQ * j:DQ * j + DQ, :].bitcast(F32)).then_inc(op_in, 16)
                            for at in k_at:
                                sp.dma_start(ks[u][j][at * DQ:(at + 1) * DQ, :].bitcast(F32),
                                             part[QS1 + DQ * j:QS1 + DQ * j + DQ, :].bitcast(F32)).then_inc(op_in, 16)

                def weights(k, u):
                    sp.wait_ge(v_ps, k + 1)
                    sp.dma_start(wpair[u % 2][:], w_qkv[(u + 2) % PAIRS]).then_inc(w_in[u % 2], 16)

                operands(0, 0)
                sp.sem_inc(out_done, 1)
                with sp.Fori(0, B) as b:
                    nxt = sp.snap((b + 1) % B)
                    for u in range(PAIRS):
                        it = sp.snap(b * PAIRS + u)
                        weights(it, u)
                        if u == 0:
                            sp.wait_ge(out_done, b * CC * 16 + 1)
                            sp.dma_start(res[:], y[bass.ds(b, 1)].rearrange("o p c n -> (o p) c n")).then_inc(r_in, 16)
                        if u == PAIRS - 1:
                            sp.dma_start(xin[:], y[bass.ds(nxt, 1)].rearrange("o p c n -> (o p) c n")).then_inc(x_in, 16)
                        operands(it + 1, (u + 1) % 2)
                    for c in range(CC):
                        sp.wait_ge(res_ok, b * CC + c + 3)
                        sp.dma_start(out[bass.ds(b, 1), c * P:(c + 1) * P, :].rearrange("o p n -> (o p) n"),
                                     res[:, c, :]).then_inc(out_done, 16)
                sp.wait_ge(out_done, B * CC * 16 + 1)
                sp.wait_ge(x_in, (B + 1) * 16)
                for u in range(2):
                    sp.wait_ge(w_in[u], (B * PAIRS // 2 + 1) * 16)
                sp.wait_ge(op_in, (B * PAIRS + 1) * MOVES)

            @block.tensor
            def _(pe):
                def chunk_product(dst, w, src, done):
                    for g in range(NH):
                        for c in range(CC):
                            mm = pe.matmul(halves(dst, g), w(c), halves(src(c), g), start=c == 0, stop=c == CC - 1)
                    mm.then_inc(done, 1)

                def qk_quarter(k, u, n):
                    g = n // 2
                    for c in range(2 * (n % 2), 2 * (n % 2) + 2):
                        mm = pe.matmul(halves(ps_p, g), wpair[u % 2][:, c, 0:P], halves(xin[:, c, :], g),
                                       start=c == 0, stop=c == CC - 1)
                    if n == 3:
                        mm.then_inc(qk_ps, 1)

                def v_tiles(k, u, tiles):
                    for m in tiles:
                        for c in range(CC):
                            mm = pe.matmul(ps_p[:, m * P:(m + 1) * P], xin[:, c, m * P:(m + 1) * P],
                                           wpair[u % 2][:, c, P:2 * P], start=c == 0, stop=c == CC - 1)
                    if m == NT - 1:
                        mm.then_inc(v_ps, 1)

                def scores(it, u, t, first_of=None):
                    for j in range(2):
                        if first_of is not None:
                            pe.wait_ge(res_ok, first_of * CC + j + 1)
                        pe.wait_ge(exp_ok, it * TILES + 2 * t + j + 1)
                        for g in range(NH):
                            mm = pe.matmul(halves(ps_s[j], g), ks[u % 2][j][:, t * P:(t + 1) * P],
                                           halves(qs[u % 2][j], g), start=True, stop=True)
                        mm.then_inc(s_ps, 1)

                def weigh(it, t):
                    if t == 0:
                        pe.wait_ge(at_ok, it + 1)
                    pe.wait_ge(vs_ok, it * NT + t + 1)
                    for g in range(NH):
                        for j in range(2):
                            mm = pe.matmul(halves(ps_o[D * j:D * j + D], g), vs[:, t % 2, j, :],
                                           halves(prob[:, t % 2, j, :], g), start=t == 0, stop=t == NT - 1)
                    mm.then_inc(o_ps, 1)

                pe.wait_ge(x_in, 16)
                pe.wait_ge(w_in[0], 16)
                for n in range(4):
                    qk_quarter(0, 0, n)
                pe.wait_ge(full_ok, 1)
                v_tiles(0, 0, range(V_MLP))
                with pe.Fori(0, B) as b:
                    def part(it, n):
                        if n == 0:
                            pe.wait_ge(mlp_in, 2 * 16)
                            pe.wait_ge(v_ok, it + 1)
                        elif n >= 2:
                            pe.wait_ge(part_ok, b * PARTS + n - 1)
                        for c in range(CC - 1):
                            mm = pe.matmul(halves(ps_p, n % 2), w1[:, c, n // 2 * P:(n // 2 + 1) * P],
                                           halves(attn[:, c, :], n % 2), start=c == 0, stop=c == CC - 2)
                        mm.then_inc(part_ps, 1)

                    for u in range(PAIRS):
                        it = pe.snap(b * PAIRS + u)
                        k, last = it + 1, u == PAIRS - 1
                        if u == 0:
                            pe.wait_ge(op_in, (it + 1) * MOVES)
                            scores(it, u, 0, first_of=b)
                            v_tiles(it, 0, range(V_MLP, NT))
                        for t in range(NT):
                            if t < NT - 1:
                                scores(it, u, t + 1)
                            elif not last:
                                pe.wait_ge(op_in, (it + 2) * MOVES)
                                scores(it + 1, u + 1, 0)
                            weigh(it, t)
                            if last and t < PARTS:
                                part(it, t)
                            n = t - (V_STEP if last else QK_STEP)
                            if 0 <= n < 4:
                                if n == 0:
                                    pe.wait_ge(v_ok, it + 1)
                                    pe.wait_ge(w_in[(u + 1) % 2], (b * 2 + (u + 1) // 2 + 1) * 16)
                                    if last:
                                        pe.wait_ge(x_in, (b + 2) * 16)
                                        pe.wait_ge(part_ok, (b + 1) * PARTS)
                                qk_quarter(k, u + 1, n)
                            elif not last and t < V_STEP + len(V_TILES):
                                if t == V_STEP:
                                    pe.wait_ge(full_ok, it + 2)
                                v_tiles(k, u + 1, V_TILES[t - V_STEP])
                    pe.wait_ge(at_ok, (b + 1) * PAIRS + 1)
                    for o in range(2):
                        for g in range(NH):
                            mm = pe.matmul(halves(ps_s[o], g), w1[:, CC - 1, o * P:(o + 1) * P],
                                           halves(attn[:, CC - 1, :], g), start=True, stop=True)
                        mm.then_inc(h_ps, 1)
                    for o in range(2, CC):
                        pe.wait_ge(z01_ok, b * 2 + o - 1)
                        chunk_product(ps_s[o % 2], lambda c: w1[:, c, o * P:(o + 1) * P],
                                      lambda c: attn[:, c, :], h_ps)
                    for c in range(CC):
                        if c == 0:
                            pe.wait_ge(full_ok, (b + 1) * PAIRS + 1)
                        if c in V_BEFORE:
                            v_tiles(0, 0, V_BEFORE[c])
                        pe.wait_ge(mish_ok, b * CC + c + 1)
                        for o in range(3):
                            if c == 0 and o < 2:
                                pe.wait_ge(z23_ok, b * 2 + o + 1)
                            for g in range(NH):
                                mm = pe.matmul(halves(r_dst[o], g), w2[:, c, o * P:(o + 1) * P], halves(hid[:, c, :], g),
                                               start=c == 0, stop=c == CC - 1)
                            if c == CC - 1:
                                mm.then_inc(r_ps, 1)
                    pe.wait_ge(res_ok, b * CC + 4)
                    chunk_product(r_dst[3], lambda c: w2[:, c, 3 * P:4 * P], lambda c: hid[:, c, :], r_ps)

            @block.scalar
            def _(act):
                act.sem_inc(exp_ok, 2)
                act.sem_inc(at_ok, 1)
                act.wait_ge(const_in, 3 * 16)

                def exps(it, t):
                    for j in range(2):
                        i = 2 * t + j
                        act.wait_ge(nms_ok, it * TILES + i + 1)
                        act.wait_ge(o_ps, it * NT + t + 1)
                        act.activation(prob[:, t % 2, j, :], ps_s[j][:], ACT.Exp, bias=nms[:, i:i + 1],
                                       scale=SCALE1, accum_out=zsum[:, i:i + 1]).then_inc(exp_ok, 1)

                def qk_high(k):
                    act.wait_ge(full_ok, k + 1)
                    if k is not FIRST:
                        act.wait_ge(op_in, k * MOVES)
                    act.activation(high[:], full[:], ACT.Identity).then_inc(high_ok, 1)

                def part(b, n):
                    act.wait_ge(part_ps, b * PARTS + n + 1)
                    o = n // 2
                    act.activation(halves(hid[:, o, :], n % 2), halves(ps_p, n % 2), ACT.Identity,
                                   bias=vecs[:, V1["b1"] + o:V1["b1"] + o + 1]).then_inc(part_ok, 1)

                qk_high(FIRST)
                with act.Fori(0, B) as b:
                    exps(act.snap(b * PAIRS), 0)
                    for u in range(PAIRS):
                        it = act.snap(b * PAIRS + u)
                        for t in range(1, NT):
                            exps(it, t)
                            if t == V_STEP and u < PAIRS - 1:
                                qk_high(it + 1)
                            if t <= PARTS and u == PAIRS - 1:
                                part(b, t - 1)
                        if u < PAIRS - 1:
                            exps(it + 1, 0)
                        act.wait_ge(o_ps, (it + 1) * NT + 2)
                        act.activation(attn[:, u, :], ps_o[:], ACT.Identity).then_inc(at_ok, 1)
                    qk_high(it + 1)
                    def hidden(c):
                        act.wait_ge(h_ps, b * CC + c + 1)
                        act.activation(hid[:, c, :], ps_s[c % 2][:], ACT.Identity,
                                       bias=vecs[:, V1["b1"] + c:V1["b1"] + c + 1]).then_inc(z23_ok, 1)

                    for first in range(0, CC, 2):
                        for c in (first, first + 1):
                            act.wait_ge(zc_ok, b * CC + c + 1)
                            act.activation(e[c % 2][:], e[c % 2][:], ACT.Exp).then_inc(e_ok, 1)
                        if first == 0:
                            hidden(2)
                        for c in (first, first + 1):
                            act.wait_ge(num_ok, b * CC + c + 1)
                            act.activation(inv[c % 2][:], num[c % 2][:], ACT.Ln, bias=two[:]).then_inc(ln_ok, 1)
                        for c in (first, first + 1):
                            act.wait_ge(ln_ok, b * CC + c + 1)
                            act.activation(inv[c % 2][:], inv[c % 2][:], ACT.Exp, scale=-1.0).then_inc(inv_ok, 1)
                        if first == 0:
                            hidden(3)

            @block.vector
            def _(dve):
                dve.sem_inc(res_ok, 2)
                dve.memset(two[:], 2.0)
                dve.sem_inc(o_ps, 2)
                dve.wait_ge(const_in, 3 * 16)

                def qk_full(k, u):
                    dve.wait_ge(qk_ps, k + 1)
                    dve.scalar_tensor_tensor(full[:], ps_p[:], vecs[:, V1["bqk"] + u:V1["bqk"] + u + 1],
                                             pos[:], ALU.add, ALU.add).then_inc(full_ok, 1)

                def qk_low(k):
                    dve.wait_ge(high_ok, k + 1)
                    dve.tensor_tensor(low[:], full[:], high[:].bitcast(F32), ALU.subtract).then_inc(low_ok, 1)

                def pair_values(k, u):
                    dve.wait_ge(v_ps, k + 1)
                    dve.tensor_tensor(vt[u % 2][:], ps_p[:].rearrange("p (m n) -> p m n", m=NT),
                                      bv[:, u * P:(u + 1) * P].rearrange("p (o n) -> p o n", o=1)
                                      .broadcast_to([P, NT, P]), ALU.add).then_inc(v_ok, 1)

                def maxima(it, t):
                    for j in range(2):
                        i = 2 * t + j
                        dve.wait_ge(s_ps, it * TILES + i + 1)
                        dve.tensor_reduce(nmax[:, i:i + 1], ps_s[j][:], AX_X, ALU.max,
                                          negate=True).then_inc(max_ok, 1)
                        dve.wait_ge(max_ok, it * TILES + i + 1)
                        dve.tensor_scalar(nms[:, i:i + 1], nmax[:, i:i + 1], SCALE1, None,
                                          ALU.mult).then_inc(nms_ok, 1)

                def scaled(it, u, t):
                    dve.wait_ge(exp_ok, it * TILES + 2 * t + 4)
                    dve.reciprocal(zinv[:, 2 * t:2 * t + 2], zsum[:, 2 * t:2 * t + 2]).then_inc(zinv_ok, 1)
                    dve.wait_ge(zinv_ok, it * NT + t + 1)
                    dve.wait_ge(o_ps, it * NT + t + 1)
                    for j in range(2):
                        last = dve.tensor_scalar(vs[:, t % 2, j, :], vt[u % 2][:, t, D * j:D * j + D],
                                                 zinv[:, 2 * t + j:2 * t + j + 1], None, ALU.mult)
                    last.then_inc(vs_ok, 1)

                qk_full(0, 0)
                qk_low(0)
                with dve.Fori(0, B) as b:
                    first_pair = dve.snap(b * PAIRS)
                    maxima(first_pair, 0)
                    pair_values(first_pair, 0)
                    for u in range(PAIRS):
                        it = dve.snap(b * PAIRS + u)
                        last = u == PAIRS - 1
                        for t in range(NT):
                            scaled(it, u, t)
                            if t == V_STEP and not last:
                                qk_full(it + 1, u + 1)
                            if t < NT - 1:
                                maxima(it, t + 1)
                            elif not last:
                                maxima(it + 1, 0)
                                pair_values(it + 1, u + 1)
                            if t == V_STEP and not last:
                                qk_low(it + 1)
                    qk_full(it + 1, 0)
                    def bounded(c):
                        if c < 2:
                            dve.wait_ge(h_ps, b * CC + c + 1)
                            dve.wait_ge(part_ok, b * PARTS + NH * (c + 1))
                            dve.tensor_tensor(hid[:, c, :], ps_s[c][:], hid[:, c, :], ALU.add).then_inc(z01_ok, 1)
                            dve.wait_ge(z01_ok, b * 2 + c + 1)
                        else:
                            dve.wait_ge(mish_ok, b * CC + c - 1)
                            dve.wait_ge(z23_ok, b * 2 + c - 1)
                        dve.tensor_scalar(e[c % 2][:], hid[:, c, :], MISH_TOP, None, ALU.min).then_inc(zc_ok, 1)

                    def numerators(two_chunks):
                        for c in two_chunks:
                            dve.wait_ge(e_ok, b * CC + c + 1)
                            dve.scalar_tensor_tensor(num[c % 2][:], e[c % 2][:], 2.0, e[c % 2][:], ALU.add,
                                                     ALU.mult).then_inc(num_ok, 1)
                        for c in two_chunks:
                            dve.wait_ge(num_ok, b * CC + c + 1)
                            dve.scalar_tensor_tensor(hid[:, c, :], num[c % 2][:], -1.0, hid[:, c, :], ALU.mult,
                                                     ALU.mult).then_inc(zn_ok, 1)

                    def quotient(c):
                        i = c % 2
                        dve.wait_ge(inv_ok, b * CC + c + 1)
                        dve.scalar_tensor_tensor(e[i][:], num[i][:], 2.0, inv[i][:], ALU.add,
                                                 ALU.mult).then_inc(newton_ok, 1)
                        dve.wait_ge(newton_ok, (b * CC + c) * 2 + 1)
                        dve.scalar_tensor_tensor(e[i][:], e[i][:], 2.0, inv[i][:], ALU.subtract,
                                                 ALU.mult).then_inc(newton_ok, 1)
                        dve.wait_ge(newton_ok, (b * CC + c) * 2 + 2)
                        dve.wait_ge(zn_ok, b * CC + c + 1)
                        dve.tensor_tensor(hid[:, c, :], hid[:, c, :], e[i][:], ALU.mult).then_inc(mish_ok, 1)

                    bounded(0)
                    bounded(1)
                    qk_low(it + 1)
                    numerators((0, 1))
                    quotient(0)
                    bounded(2)
                    quotient(1)
                    bounded(3)
                    numerators((2, 3))
                    quotient(2)
                    quotient(3)
                    dve.wait_ge(r_in, (b + 1) * 16)
                    for c in range(CC):
                        dve.wait_ge(r_ps, b * CC + c + 1)
                        dve.scalar_tensor_tensor(res[:, c, :], r_dst[c][:], vecs[:, V1["b2"] + c:V1["b2"] + c + 1],
                                                 res[:, c, :], ALU.add, ALU.add).then_inc(res_ok, 1)


def build(nc, x, w0_qkv, w0_out, vec0, w_sp, b_sp, w_se1, b_se1, w_se2, ident, w1_qkv, w1, w2, vec1, bv1, pos, out):
    mask_d = nc.dram_tensor("mask_rows", (HEADS, 4, N), F32, kind="Internal").ap()
    y = nc.dram_tensor("layer0_out", (B, P, CC, N), F32, kind="Internal").ap()
    layer0(nc, x, w0_qkv, w0_out, vec0, w_sp, b_sp, w_se1, b_se1, w_se2, ident, mask_d, y)
    layer1(nc, y, w1_qkv, w1, w2, vec1, bv1, pos, out)


def kernel(**inputs):
    import numpy as np
    import concourse.bacc as bacc
    from concourse.bass_utils import run_bass_kernel_spmd

    def arr(name):
        return np.asarray(inputs[name])

    def turned(w):
        return np.ascontiguousarray(w.T.reshape(CC, P, w.shape[0]).transpose(1, 0, 2))

    def columns(v):
        return v.reshape(-1, P).T

    l0 = {k: arr(f"L0_conv_{k}") for k in ("Wq", "Wk", "Wv", "Wo", "Wsp", "Wse1", "Wse2", "bq", "bk", "bv", "bo",
                                            "bsp", "bse1", "bse2", "gamma", "beta")}
    l1 = {k: arr(f"L1_conv_{k}") for k in ("PE", "Wq", "Wk", "Wv", "W1", "W2", "bq", "bk", "bv", "b1", "b2")}

    def by_pair(*ws):
        parts = [turned(w).reshape(P, CC, PAIRS, -1).transpose(2, 0, 1, 3) for w in ws]
        return np.ascontiguousarray(np.concatenate(parts, axis=3))

    bqk = np.concatenate([l1["bq"].reshape(PAIRS, QS1), l1["bk"].reshape(PAIRS, QS1)], axis=1).T
    given = {
        "x": np.ascontiguousarray(arr("x").reshape(B, CC, P, N).transpose(0, 2, 1, 3)),
        "w0_qkv": by_pair(l0["Wq"], l0["Wk"], l0["Wv"]),
        "w0_out": turned(l0["Wo"]),
        "vec0": np.ascontiguousarray(np.concatenate([columns(l0[k]) for k in V0], axis=1)),
        "w_sp": turned(l0["Wsp"]),
        "b_sp": np.ascontiguousarray(l0["bsp"].reshape(HEADS, 1)),
        "w_se1": turned(l0["Wse1"]),
        "b_se1": np.ascontiguousarray(l0["bse1"].reshape(SE, 1)),
        "w_se2": np.ascontiguousarray(l0["Wse2"].T),
        "ident": np.eye(P, dtype=np.float32),
        "w1_qkv": by_pair(l1["Wq"], l1["Wk"], l1["Wv"]),
        "w1": turned(l1["W1"]),
        "w2": turned(l1["W2"]),
        "vec1": np.ascontiguousarray(np.concatenate([bqk, columns(l1["b1"]), columns(l1["b2"])], axis=1)),
        "bv1": np.ascontiguousarray(l1["bv"]),
        "pos": np.ascontiguousarray(np.concatenate([l1["PE"].reshape(DQ, N)] * (P // DQ), axis=0)),
    }
    nc = bacc.Bacc("TRN2", target_bir_lowering=False, num_devices=1)
    args = [nc.dram_tensor(f"in_{k}", v.shape, F32, kind="ExternalInput").ap() for k, v in given.items()]
    out = nc.dram_tensor("out_0", (B, C, N), F32, kind="ExternalOutput").ap()
    build(nc, *args, out)
    r = run_bass_kernel_spmd(nc, [{f"in_{k}": v for k, v in given.items()}], core_ids=[0])
    return r.results[0]["out_0"].reshape(B, C, H, W)
```
